# Optimizing a Trainium2 kernel written in Bass

```python
import numpy as np
import jax
import jax.numpy as jnp

def _softmax(x, axis=-1):
    return jax.nn.softmax(x, axis=axis)

def _gelu(x):
    return jax.nn.gelu(x, approximate=True)

def _silu(x):
    return jax.nn.silu(x)

def _sigmoid(x):
    return jax.nn.sigmoid(x)

def _layernorm(x, axis=-1, eps=1e-05):
    m = jnp.mean(x, axis=axis, keepdims=True)
    v = jnp.var(x, axis=axis, keepdims=True)
    return (x - m) / jnp.sqrt(v + eps)

def _scatter_add(tgt, idx, src, axis=0):
    return tgt.at[idx].add(src)

def _segment_sum(src, seg, n):
    return jax.ops.segment_sum(src, seg, n)
kernel_name = 'mk_xattn_ffn_d1_seqx_r4_6da7fd'

def setup_inputs(seed: int=0):
    np.random.seed(seed)
    _w = jnp.asarray

    def _rec_inputs():
        import jax
        import jax.numpy as jnp
        _rk = jax.random.key(seed)
        x = -0.0002928 + 1 * jax.random.normal(jax.random.fold_in(_rk, 1), (16, 256, 512), jnp.float32)
        _lenS = 256 - jax.random.randint(jax.random.fold_in(_rk, 7), (16,), 0, max(1, 256 // 4) + 1, jnp.int32)
        _lenS2 = 256 - jax.random.randint(jax.random.fold_in(_rk, 8), (16,), 0, max(1, 256 // 4) + 1, jnp.int32)
        _ctx_2048P = jax.random.normal(jax.random.fold_in(_rk, 11), (16, 16, 512), jnp.float32)
        _ctx_2048c = jax.random.dirichlet(jax.random.fold_in(_rk, 511), 0.3 * jnp.ones((16,), jnp.float32), (16, 256))
        _ctx_2048t = jnp.einsum('bsk,bkd->bsd', _ctx_2048c, _ctx_2048P)
        _ctx_2048t = _ctx_2048t * jax.lax.rsqrt(jnp.mean(jnp.square(_ctx_2048t)) + 1e-12) * 0.953939
        ctx_2048 = -1.39393e-06 + 0.999914 * (_ctx_2048t + 0.3 * jax.random.normal(jax.random.fold_in(_rk, 611), (16, 256, 512), jnp.float32))
        _validS = jnp.arange(256)[None, :] < _lenS[:, None]
        _validS2 = jnp.arange(256)[None, :] < _lenS2[:, None]
        _causal = jnp.tril(jnp.ones((256, 256), dtype=bool))
        mask_Bx1x2048_fk1 = jnp.where(jnp.ones((16, 1, 512), dtype=bool), 1.0, 0.0).astype(jnp.float32)
        return (x, ctx_2048, mask_Bx1x2048_fk1)
    x, ctx_2048, mask_Bx1x2048_fk1 = _rec_inputs()

    def _L0_xattn_setup():
        import math
        import jax, jax.numpy as jnp
        import numpy as np
        SIZE = 256
        HEADS = 16
        HEAD_DIM = SIZE // HEADS
        B, T, S = (2, 512, 512)
        NEG = 1000000.0
        key = jax.random.key(seed)
        ks = jax.random.split(key, 10)
        target = jax.random.normal(ks[0], (B, SIZE, T), dtype=jnp.float32)
        source = jax.random.normal(ks[1], (B, SIZE, S), dtype=jnp.float32)
        target_mask = (jax.random.uniform(ks[2], (B, 1, T)) > 0.1).astype(jnp.float32)
        source_mask = (jax.random.uniform(ks[3], (B, 1, S)) > 0.1).astype(jnp.float32)
        scale = 1.0 / math.sqrt(SIZE)
        Wq = jax.random.normal(ks[4], (SIZE, SIZE), dtype=jnp.float32) * scale
        Wk = jax.random.normal(ks[5], (SIZE, SIZE), dtype=jnp.float32) * scale
        Wv = jax.random.normal(ks[6], (SIZE, SIZE), dtype=jnp.float32) * scale
        bq = jax.random.normal(ks[7], (SIZE,), dtype=jnp.float32) * 0.01
        bk = jax.random.normal(ks[8], (SIZE,), dtype=jnp.float32) * 0.01
        bv = jax.random.normal(ks[9], (SIZE,), dtype=jnp.float32) * 0.01
        return {'target': target, 'source': source, 'target_mask': target_mask, 'source_mask': source_mask, 'Wq': Wq, 'bq': bq, 'Wk': Wk, 'bk': bk, 'Wv': Wv, 'bv': bv}
    _L0_xattn_all = _L0_xattn_setup()
    _L0_xattn_in = {k: v for k, v in _L0_xattn_all.items() if k in ('Wq', 'bq', 'Wk', 'bk', 'Wv', 'bv')}
    del _L0_xattn_all

    def _L0_ffn_setup():
        import jax, jax.numpy as jnp
        import numpy as np
        HIDDEN = 512
        INTER = 1376
        LUT_SIZE = 16

        def _ghost_linear(x, idx, lut):
            w = lut[idx]
            return jnp.einsum('bsh,oh->bso', x, w)
        key = jax.random.key(seed)
        k_x, k_lut, k_g, k_u, k_d = jax.random.split(key, 5)
        x = jax.random.normal(k_x, (2, 1024, HIDDEN), dtype=jnp.float32)
        lut = jax.random.normal(k_lut, (LUT_SIZE,), dtype=jnp.float32) * 0.02
        gate_idx = jax.random.randint(k_g, (INTER, HIDDEN), 0, LUT_SIZE, dtype=jnp.int32)
        up_idx = jax.random.randint(k_u, (INTER, HIDDEN), 0, LUT_SIZE, dtype=jnp.int32)
        down_idx = jax.random.randint(k_d, (HIDDEN, INTER), 0, LUT_SIZE, dtype=jnp.int32)
        return {'x': x, 'lut': lut, 'gate_idx': gate_idx, 'up_idx': up_idx, 'down_idx': down_idx}
    _L0_ffn_all = _L0_ffn_setup()
    _L0_ffn_in = {k: v for k, v in _L0_ffn_all.items() if k in ('lut', 'gate_idx', 'up_idx', 'down_idx')}
    del _L0_ffn_all
    return {'x': x, 'ctx_2048': ctx_2048, 'mask_Bx1x2048_fk1': mask_Bx1x2048_fk1, 'L0_xattn_Wq': _L0_xattn_in['Wq'], 'L0_xattn_bq': _L0_xattn_in['bq'], 'L0_xattn_Wk': _L0_xattn_in['Wk'], 'L0_xattn_bk': _L0_xattn_in['bk'], 'L0_xattn_Wv': _L0_xattn_in['Wv'], 'L0_xattn_bv': _L0_xattn_in['bv'], 'L0_ffn_lut': _L0_ffn_in['lut'], 'L0_ffn_gate_idx': _L0_ffn_in['gate_idx'], 'L0_ffn_up_idx': _L0_ffn_in['up_idx'], 'L0_ffn_down_idx': _L0_ffn_in['down_idx']}

def reference(x, ctx_2048, mask_Bx1x2048_fk1, L0_xattn_Wq, L0_xattn_bq, L0_xattn_Wk, L0_xattn_bk, L0_xattn_Wv, L0_xattn_bv, L0_ffn_lut, L0_ffn_gate_idx, L0_ffn_up_idx, L0_ffn_down_idx):
    import jax
    import jax.numpy as jnp

    def _L0_xattn_ref(target, source, target_mask, source_mask, Wq, bq, Wk, bk, Wv, bv):
        import math
        import jax, jax.numpy as jnp
        import numpy as np
        SIZE = 256
        HEADS = 16
        HEAD_DIM = SIZE // HEADS
        B, T, S = (2, 512, 512)
        NEG = 1000000.0
        b, _, t = target.shape
        s = source.shape[-1]
        q = jnp.einsum('oc,bct->bot', Wq, target) + bq[None, :, None]
        k = jnp.einsum('oc,bcs->bos', Wk, source) + bk[None, :, None]
        v = jnp.einsum('oc,bcs->bos', Wv, source) + bv[None, :, None]
        q = q.reshape(b, HEADS, HEAD_DIM, t)
        k = k.reshape(b, HEADS, HEAD_DIM, s)
        v = v.reshape(b, HEADS, HEAD_DIM, s)
        dot = jnp.einsum('bhdt,bhds->bhts', q, k) / math.sqrt(HEAD_DIM)
        mask = target_mask[:, :, :, None] * source_mask[:, :, None, :]
        dot = mask * dot - (1.0 - mask) * NEG
        amap = jax.nn.softmax(dot, axis=-1) * mask
        out = jnp.einsum('bhts,bhds->bhdt', amap, v)
        return out.reshape(b, HEADS * HEAD_DIM, t)

    def _L0_ffn_ref(x, lut, gate_idx, up_idx, down_idx):
        import jax, jax.numpy as jnp
        import numpy as np
        HIDDEN = 512
        INTER = 1376
        LUT_SIZE = 16

        def _ghost_linear(x, idx, lut):
            w = lut[idx]
            return jnp.einsum('bsh,oh->bso', x, w)
        gate = _ghost_linear(x, gate_idx, lut)
        up = _ghost_linear(x, up_idx, lut)
        h = jax.nn.silu(gate) * up
        return _ghost_linear(h, down_idx, lut)
    x = x + _L0_xattn_ref(_layernorm(x, axis=-1), ctx_2048, mask_Bx1x2048_fk1, mask_Bx1x2048_fk1, L0_xattn_Wq, L0_xattn_bq, L0_xattn_Wk, L0_xattn_bk, L0_xattn_Wv, L0_xattn_bv)
    x = x + _L0_ffn_ref(_layernorm(x, axis=-1), L0_ffn_lut, L0_ffn_gate_idx, L0_ffn_up_idx, L0_ffn_down_idx)
    return x

_drawn_inputs = setup_inputs


def setup_inputs(seed=0):
    import zlib

    import numpy as np

    out = dict(_drawn_inputs(seed))
    spreads = {}
    factors = {'L0_xattn_bv': 5.816}
    for name, (base, spread) in spreads.items():
        noise = np.random.default_rng([zlib.crc32(name.encode()), seed]).standard_normal(out[name].shape)
        drawn = base * np.exp(spread * noise) if base else spread * noise
        out[name] = jnp.asarray(drawn.astype(out[name].dtype))
    for name, factor in factors.items():
        out[name] = (out[name] * factor).astype(out[name].dtype)
    return out
```

```python
from contextlib import ExitStack

import concourse.bass as bass
from concourse import mybir

ALU = mybir.AluOpType
ACT = mybir.ActivationFunctionType
X = mybir.AxisListType.X
F32 = mybir.dt.float32
F16 = mybir.dt.float16
BF16 = mybir.dt.bfloat16
I32 = mybir.dt.int32
U32 = mybir.dt.uint32

P = 128
B, C, T = 16, 256, 512
H, D = 16, 16
INTER, LUT = 1376, 16
KT = T // P
IT = -(-INTER // P)
ILAST = INTER - (IT - 1) * P
GATE0, UP0, DOWN0 = 0, KT * INTER, 2 * KT * INTER
WCOLS = DOWN0 + IT * T
WB = WCOLS // B
CH = WB // 4
NEG = 1.0e6
EPS = 1e-5
SLOTS = 6
QPART = (0, 0, 1, 0, 2, 1)
KPART = (0, 1, 0, 2, 0, 1)
MROW = SLOTS * D
XROW = MROW + SLOTS
SROWS = XROW + 2
DW = D + 1
GT = 512
GTT = GT // P

JOBS = {0: ["L0"], 1: ["L1"], 2: ["L2"], 3: ["T", "L3"], 4: ["q"], 5: ["k"], 6: ["v"], 7: ["T"],
        8: ["L4"], 9: ["L5"], 10: ["L6"], 11: ["T", "L7"], 12: ["q"], 13: ["k"], 14: ["v"], 15: ["T"]}
STEPS = 16
ORDER = [(g, name) for g in range(STEPS) for name in JOBS[g]]
LAST_ORDER = [(g, name) for g, name in ORDER if name[0] == "L" or (name == "T" and g < 15)]
NJ = len(ORDER)
AHEAD = 5
FIRST = ["q", "k", "v", "q", "k", "v", "T"]
PER = {c: sum(name[0] == c for _, name in ORDER) for c in "LqkvT"}


def wait(eng, sem, value):
    if not (isinstance(value, int) and value <= 0):
        eng.wait_ge(sem, value)


def settle(eng, sem):
    eng.sem_inc(sem, 1)


def batches(eng, body):
    body(0, 0)
    body(1, 1)
    with eng.Fori(1, B // 2 - 1) as pair:
        body(pair * 2, 0)
        body(pair * 2 + 1, 1)
    body(B - 2, 0, load=False)
    body(B - 1, 1, load=False, last=True)


def jobs_of(last):
    return LAST_ORDER if last else ORDER


def ordinal(b, k, last=False):
    order, back = (ORDER, b - 1) if k < 0 else (jobs_of(last), b)
    kind = order[k][1][0]
    here = sum(name[0] == kind for _, name in order[:k % len(order) + 1])
    return kind, FIRST.count(kind) + PER[kind] * back + here


def build(nc, x, ctx, mask, wq, bq, wk, bk, wv, bv, lut, idx, out):
    xmid = nc.dram_tensor("xmid", [B, C, T], F32, kind="Internal").ap()
    mask_rows = nc.dram_tensor("mask_rows", [B, 2, SLOTS, T], BF16, kind="Internal").ap()
    den_rows = nc.dram_tensor("den_rows", [2, H // 2, T], F32, kind="Internal").ap()
    with ExitStack() as keep:
        w_hi = keep.enter_context(nc.sbuf_tensor("w_hi", [P, WCOLS], F16))
        w_lo = keep.enter_context(nc.sbuf_tensor("w_lo", [P, WCOLS], F16))
        scales = keep.enter_context(nc.sbuf_tensor("scales", [P, 4], F32))
        ident16 = keep.enter_context(nc.sbuf_tensor("ident16", [P, P], F16))
        with ExitStack() as st:
            attention(nc, st, x, ctx, mask, wq, bq, wk, bk, wv, bv, lut, idx, xmid, mask_rows, den_rows,
                      w_hi, w_lo, scales, ident16)
        with ExitStack() as st:
            ffn(nc, st, xmid, out, w_hi, w_lo, scales, ident16)


def attention(nc, st, x, ctx, mask, wq, bq, wk, bk, wv, bv, lut, idx, xmid, mask_rows, den_rows,
              w_hi, w_lo, scales, ident16):
    def sb(name, shape, dt=F32):
        return st.enter_context(nc.sbuf_tensor(name, shape, dt))

    def sem(name):
        return st.enter_context(nc.semaphore(name))

    qs = sb("qs", [P, 2, 8, T], BF16)
    ks = sb("ks", [P, 2, 8, T], BF16)
    vt = sb("vt", [P, 2, 2, 4, 8, DW])
    probs = sb("probs", [P, 2, 4, T])
    x_in = sb("x_in", [P, 2, T])
    c_in = sb("c_in", [P, 2, T])
    xn = sb("xn", [P, 2, T])
    cm = sb("cm", [P, 2, T])
    mb = sb("mb", [P, 2, T])
    mcol = sb("mcol", [P, 2, 4])
    full = sb("full", [P, T])
    rest = sb("rest", [P, T])
    qp = sb("qp", [P, 3, T], BF16)
    kp = sb("kp", [P, 3, T], BF16)
    o_sb = sb("o_sb", [P, 2, T])
    num = sb("num", [P, 2, T])
    rb = sb("rb", [P, T])
    xr = sb("xr", [P, T])
    den = sb("den", [64, 2, 64])
    rden = sb("rden", [64, 2, 64])
    tm = sb("tm", [64, 2, 64])
    idx_in = sb("idx_in", [P, WB], I32)
    idxf = sb("idxf", [P, CH], F16)
    onehot = sb("onehot", [P, 2, LUT, CH], F16)
    diag = sb("diag", [P, 2, LUT, P], F16)
    ident = sb("ident", [P, P])
    wq_sb = sb("wq_sb", [P, 2, C])
    wk_sb = sb("wk_sb", [P, 2, C])
    wv_sb = sb("wv_sb", [P, 2, C])
    b_sb = sb("b_sb", [P, 4])
    bv_b = sb("bv_b", [P, C])
    lut_b = sb("lut_b", [P, 5, LUT])
    lut16 = sb("lut16", [P, LUT], F16)
    lt = sb("lt", [P, 8])
    stats = sb("stats", [P, 2, 6])
    mv = sb("mv", [P, 2, 2])
    ve = sb("ve", [P, 2])
    mhalf = sb("mhalf", [P, 2])
    rstd = sb("rstd", [P, 2])
    mx = sb("mx", [P, 2, 16])
    mt = sb("mt", [16, 2, 2, P], BF16)

    ps_s = st.enter_context(nc.psum_tensor("ps_s", [P, 2, 512], F32))
    ps_t = st.enter_context(nc.psum_tensor("ps_t", [P, 2, 512], F32))
    ps_o = st.enter_context(nc.psum_tensor("ps_o", [P, 2, 512], F32))
    ps_j = st.enter_context(nc.psum_tensor("ps_j", [P, 2, 512], F32))

    settled = sem("settled")
    const_in = sem("const_in")
    small_in = sem("small_in")
    mask_in = sem("mask_in")
    mrow_out = sem("mrow_out")
    ident_rdy = sem("ident_rdy")
    half_rdy = sem("half_rdy")
    mem_rdy = sem("mem_rdy")
    pool_chain = sem("pool_chain")
    diag_rdy = sem("diag_rdy")
    dv = sem("dv")
    inp = sem("inp")
    idx_sem = sem("idx_sem")
    idx_used = sem("idx_used")
    var_rdy = sem("var_rdy")
    rstd_rdy = sem("rstd_rdy")
    xn_rdy = sem("xn_rdy")
    cm_rdy = sem("cm_rdy")
    parts_rdy = sem("parts_rdy")
    stack_in = [sem("stack_in0"), sem("stack_in1")]
    s_done = sem("s_done")
    mx_done = sem("mx_done")
    t_done = sem("t_done")
    exp_done = sem("exp_done")
    pv_done = sem("pv_done")
    job_done = sem("job_done")
    emptied = {"q": sem("q_out"), "k": sem("k_out"), "v": sem("v_out"), "T": sem("max_out"), "L": sem("w_out")}
    max_in = sem("max_in")
    hot_rdy = sem("hot_rdy")
    o_rdy = sem("o_rdy")
    gathered = [sem("gathered0"), sem("gathered1")]
    tm_in = sem("tm_in")
    den_sem = sem("den_sem")
    rden_rdy = sem("rden_rdy")
    bounce = sem("bounce")
    rb_in = sem("rb_in")
    res_rdy = sem("res_rdy")
    sum_rdy = sem("sum_rdy")
    stored = sem("stored")

    NSTACK = 16 * (2 * SLOTS + 2)

    def jobs_through(b, k):
        return len(FIRST) + NJ * b + k + 1

    with nc.Block() as block:

        @block.sync
        def _(sp):
            def load_inputs(b, par):
                sp.dma_start(x_in[:], x[bass.ds(b, 1), :, :].rearrange("o (t p) f -> p (o t) f", p=P)).then_inc(inp, 16)
                sp.dma_start(c_in[:], ctx[bass.ds(b, 1), :, :].rearrange("o (t p) f -> p (o t) f", p=P)).then_inc(inp, 16)
                sp.dma_start(mb[:, par, :], mask[bass.ds(b, 1), 0, :].to_broadcast([P, T])).then_inc(inp, 16)
                with nc.allow_non_contiguous_dma("512 mask values, positions to the partitions"):
                    sp.dma_start(mcol[:, par, :], mask[bass.ds(b, 1), 0, :].rearrange("o (j p) -> p (o j)", p=P)
                                 ).then_inc(inp, 16)

            def stack(b, half, readers):
                sp.wait_ge(parts_rdy, b * 4 + 2 * half + 2)
                settle(sp, settled)
                wait(sp, t_done, readers)
                for slot in range(SLOTS):
                    for dst, src, part in ((qs, qp, QPART[slot]), (ks, kp, KPART[slot])):
                        sp.dma_start(dst[slot * D:(slot + 1) * D, half, :, :],
                                     src[:, part, :]).then_inc(stack_in[half], 16)
                for side, dst in ((0, qs), (1, ks)):
                    rows = mask_rows[bass.ds(b, 1), side, :, :].rearrange("o s t -> (o s) t")
                    sp.dma_start(dst[MROW:XROW, half, :, :],
                                 rows.unsqueeze(1).to_broadcast([SLOTS, 8, T])).then_inc(stack_in[half], 16)

            def gather(b, s):
                if isinstance(b, int) and 4 * b + s == 0:
                    return
                half, g2 = ((s - 1) % 4) // 2, (s - 1) % 2
                sp.wait_ge(o_rdy, b * 4 + s)
                settle(sp, settled)
                wait(sp, res_rdy, b * 2 + (-2, -1, -1, 0)[s])
                for i in range(4):
                    sp.dma_start(num[64 * g2 + 16 * i:64 * g2 + 16 * i + 16, half, :],
                                 o_sb[32 * i:32 * i + 16, g2, :]).then_inc(gathered[g2], 16)
                sp.dma_start(den[32 * g2:32 * g2 + 32, half, :], o_sb[D:P:32, g2, :]).then_inc(gathered[g2], 16)

            def max_rows(n, half, g2):
                sp.wait_ge(emptied["T"], n + 1)
                for part in range(2):
                    sp.dma_start(qs[XROW + part:XROW + part + 1, half, 4 * g2:4 * g2 + 4, :],
                                 mt[:, g2, part, :]).then_inc(max_in, 16)

            load_inputs(0, 0)
            for dst, src in ((wq_sb, wq), (wk_sb, wk), (wv_sb, wv)):
                sp.dma_start(dst[:], src.rearrange("(k p) o -> p k o", p=P)).then_inc(const_in, 16)
            sp.dma_start(b_sb[:, 0:2], bq).then_inc(const_in, 16)
            sp.dma_start(b_sb[:, 2:4], bk).then_inc(const_in, 16)
            sp.dma_start(bv_b[:], bv.to_broadcast([P, C])).then_inc(const_in, 16)
            sp.dma_start(idx_in[:], idx[:, 0, :]).then_inc(idx_sem, 16)
            sp.wait_ge(mem_rdy, 1)
            sp.wait_ge(mrow_out, 2 * 16 * SLOTS)
            stack(0, 0, 0)
            sp.wait_ge(xn_rdy, 1)
            sp.wait_ge(cm_rdy, 1)
            load_inputs(1, 1)
            max_rows(0, 0, 0)

            def body(b, par, load=True, last=False):
                stack(b, 1, b * 64)
                gather(b, 0)
                max_rows(b * 4 + 1, 0, 1)
                gather(b, 1)
                max_rows(b * 4 + 2, 1, 0)
                if load:
                    sp.wait_ge(xn_rdy, b + 2)
                    settle(sp, settled)
                    sp.wait_ge(cm_rdy, b + 2)
                    settle(sp, settled)
                    sp.wait_ge(emptied["v"], b * 2 + 2)
                    settle(sp, settled)
                    load_inputs(b + 2, par)
                if not last:
                    sp.wait_ge(idx_used, b * 4 + 4)
                    settle(sp, settled)
                    sp.dma_start(idx_in[:], idx[:, bass.ds(b + 1, 1), :]).then_inc(idx_sem, 16)
                    stack(b + 1, 0, b * 64 + 32)
                gather(b, 2)
                max_rows(b * 4 + 3, 1, 1)
                gather(b, 3)
                if not last:
                    max_rows(b * 4 + 4, 0, 0)

            batches(sp, body)
            gather(B, 0)

        @block.gpsimd
        def _(pool):
            count = [0]

            def link(ins):
                count[0] += 1
                ins.then_inc(pool_chain, 1)
                pool.wait_ge(pool_chain, count[0])

            pool.dma_start(lut_b[:, 0, :], lut.to_broadcast([P, LUT])).then_inc(small_in, 16)
            mrow, mres = num[0:B, 0, :], rb[0:B, :]
            mpart = o_sb[0:B, :, :].rearrange("p a t -> p (a t)").bitcast(BF16)[:, 0:3 * T] \
                .rearrange("p (s t) -> p s t", t=T)
            pool.dma_start(mrow, mask.rearrange("b o t -> b (o t)")).then_inc(mask_in, 16)
            pool.memset(ident[:], 0.0).then_inc(ident_rdy, 1)
            pool.wait_ge(ident_rdy, 1)
            pool.affine_select(out=ident[:], in_=ident[:], compare_op=ALU.not_equal, fill=1.0, base=0,
                               pattern=[[-1, P]], channel_multiplier=1).then_inc(ident_rdy, 1)
            pool.memset(mhalf[:], -0.5).then_inc(half_rdy, 1)

            def mask_context(b, par, jobs):
                pool.wait_ge(inp, (b + 1) * 64)
                wait(pool, job_done, jobs)
                for t in range(2):
                    ins = pool.tensor_tensor(cm[:, t, :], c_in[:, t, :], mb[:, par, :], ALU.mult)
                ins.then_inc(cm_rdy, 1)

            def inv_std(b):
                pool.wait_ge(var_rdy, b + 1)
                pool.tensor_tensor(rstd[:], ve[:], mhalf[:], ALU.pow).then_inc(rstd_rdy, 1)

            pool.wait_ge(half_rdy, 1)
            mask_context(0, 0, 0)
            inv_std(0)
            pool.wait_ge(mask_in, 16)
            for side in range(2):
                if side == 0:
                    link(pool.tensor_copy(mres, mrow))
                else:
                    link(pool.tensor_scalar(mres, mrow, -1.0, 4.0 * NEG, ALU.add, ALU.mult))
                for part in range(3):
                    link(pool.tensor_copy(mpart[:, part, :], mres))
                    if part < 2:
                        link(pool.tensor_tensor(mres, mres, mpart[:, part, :], ALU.subtract))
                for slot in range(SLOTS):
                    part = (QPART, KPART)[side][slot]
                    pool.dma_start(mask_rows[:, side, slot, :], mpart[:, part, :]).then_inc(mrow_out, 16)
                pool.wait_ge(mrow_out, 16 * SLOTS * (side + 1))

            def finish(b, half):
                u = b * 2 + half
                pool.wait_ge(rden_rdy, u + 1)
                settle(pool, settled)
                pool.dma_start(den_rows[half, :, :].rearrange("h (c t) -> (h c) t", t=64),
                               rden[:, half, :]).then_inc(bounce, 16)
                wait(pool, stored, u * 16)
                settle(pool, settled)
                pool.dma_start(xr[:], x[bass.ds(b, 1), half * P:(half + 1) * P, :]
                               .rearrange("o p f -> (o p) f")).then_inc(rb_in, 16)
                pool.wait_ge(bounce, (u + 1) * 16)
                settle(pool, settled)
                pool.dma_start(rb[:], den_rows[half, :, :].unsqueeze(1).to_broadcast([8, D, T])
                               ).then_inc(rb_in, 16)
                pool.wait_ge(rb_in, (u + 1) * 32)
                for p2 in range(2):
                    pool.wait_ge(gathered[p2], (u + 1) * GATHER)
                pool.tensor_tensor(rb[:], num[:, half, :], rb[:], ALU.mult).then_inc(res_rdy, 1)
                pool.wait_ge(res_rdy, u + 1)
                pool.tensor_tensor(xr[:], xr[:], rb[:], ALU.add).then_inc(sum_rdy, 1)
                pool.wait_ge(sum_rdy, u + 1)
                settle(pool, settled)
                pool.dma_start(xmid[bass.ds(b, 1), half * P:(half + 1) * P, :].rearrange("o p f -> (o p) f"),
                               xr[:]).then_inc(stored, 16)

            def load_tm(b, par):
                m8 = mask[bass.ds(b, 1), 0, :].rearrange("o (c t) -> o c t", t=64)
                pool.dma_start(tm[:, par, :], m8.to_broadcast([8, 8, 64])).then_inc(tm_in, 16)

            def body(b, par, load=True, last=False):
                if not last:
                    mask_context(b + 1, 1 - par, jobs_through(b, -1))
                    inv_std(b + 1)
                load_tm(b, par)
                if not (isinstance(b, int) and b == 0):
                    finish(b - 1, 1)
                finish(b, 0)

            batches(pool, body)
            finish(B - 1, 1)
            pool.wait_ge(stored, 16 * 2 * B)

        @block.scalar
        def _(act):
            act.wait_ge(mem_rdy, 1)
            act.wait_ge(mrow_out, 2 * 16 * SLOTS)

            def take_out(n, p2, before):
                act.wait_ge(pv_done, n * 4 + 4)
                wait(act, gathered[p2], before * GATHER)
                act.activation(o_sb[:, p2, :], ps_o[:, p2, :], ACT.Copy).then_inc(o_rdy, 1)

            def body(b, par, load=True, last=False):
                order = jobs_of(last)
                for g in range(STEPS):
                    for i in range(4):
                        m = 4 * g + i
                        act.wait_ge(t_done, b * 64 + (m + 1))
                        if i == 0:
                            wait(act, pv_done, b * 16 + (g - 1))
                        act.activation(probs[:, g % 2, i, :], ps_t[:, m % 2, :], ACT.Exp,
                                       scale=0.25).then_inc(exp_done, 1)
                    s = g // 4
                    p2, before = (s - 1) % 2, b * 2 + (-1, 0, 0, 1)[s]
                    if not (isinstance(b, int) and b == 0 and s == 0):
                        if g % 4 == 1:
                            take_out(b * 4 + (s - 1), p2, before)
                    for k, (gk, name) in enumerate(order):
                        if gk == g and name[0] == "L":
                            c, part = int(name[1]) // 2, int(name[1]) % 2
                            act.wait_ge(job_done, jobs_through(b, k))
                            w = (w_hi, w_lo)[part]
                            act.activation(w[:, bass.ds(b * WB + c * CH, CH)], ps_j[:, k % 2, 0:CH],
                                           ACT.Copy).then_inc(emptied["L"], 1)

            batches(act, body)
            take_out(4 * B - 1, 1, 2 * B - 1)

        @block.vector
        def _(dve):
            class Chain:
                base, per, b, k = 0, 0, 0, 0

            def link(ins):
                Chain.k += 1
                ins.then_inc(dv, 1)
                dve.wait_ge(dv, Chain.b * Chain.per + (Chain.base + Chain.k))

            dve.memset(ks[96:P, :, :, :], 1.0)
            dve.memset(qs[96:P, :, :, :], 0.0)
            dve.memset(vt[:], 1.0)
            dve.memset(lt[:], 0.0)
            dve.memset(ps_o[:], 0.0).then_inc(mem_rdy, 1)

            def norm_stats(b):
                dve.wait_ge(inp, (b + 1) * 64)
                for t in range(2):
                    ins = dve.bn_stats(stats[:, t, :], x_in[:, t, :])
                link(ins)
                settle(dve, settled)
                for t in range(2):
                    ins = dve.bn_aggr(mv[:, t, :], stats[:, t, :])
                link(ins)
                dve.tensor_scalar(ve[:], mv[:, :, 1], EPS, None, ALU.add).then_inc(var_rdy, 1)

            def normalise(b, jobs):
                dve.wait_ge(rstd_rdy, b + 1)
                wait(dve, job_done, jobs)
                for t in range(2):
                    ins = dve.tensor_scalar(xn[:, t, :], x_in[:, t, :], mv[:, t, 0:1], rstd[:, t:t + 1],
                                            ALU.subtract, ALU.mult)
                ins.then_inc(xn_rdy, 1)

            def cut(parts, stage):
                if stage == 0:
                    link(dve.tensor_copy(parts[:, 0, :], full[:]))
                if stage == 1:
                    link(dve.tensor_tensor(rest[:], full[:], parts[:, 0, :], ALU.subtract))
                if stage == 2:
                    link(dve.tensor_copy(parts[:, 1, :], rest[:]))
                if stage == 3:
                    dve.tensor_tensor(parts[:, 2, :], rest[:], parts[:, 1, :], ALU.subtract
                                      ).then_inc(parts_rdy, 1)

            def take_q(b, par, half, job, slot):
                dve.wait_ge(job_done, job)
                if half == 0:
                    wait(dve, stack_in[1], b * NSTACK)
                else:
                    dve.wait_ge(stack_in[0], (b + 1) * NSTACK)
                dve.scalar_tensor_tensor(out=full[:], in0=ps_j[:, slot, :], scalar=b_sb[:, half:half + 1],
                                         in1=mb[:, par, :], op0=ALU.add, op1=ALU.mult).then_inc(emptied["q"], 1)
                dve.wait_ge(emptied["q"], b * 2 + (half + 1))

            def take_k(b, par, half, job, slot):
                dve.wait_ge(job_done, job)
                dve.scalar_tensor_tensor(out=full[:], in0=mb[:, par, :], scalar=b_sb[:, 2 + half:3 + half],
                                         in1=ps_j[:, slot, :], op0=ALU.mult, op1=ALU.add
                                         ).then_inc(emptied["k"], 1)
                dve.wait_ge(emptied["k"], b * 2 + (half + 1))

            def take_v(b, par, half, job, slot):
                dve.wait_ge(job_done, job)
                wait(dve, pv_done, (b - 1) * 16)
                for j in range(4):
                    ins = dve.scalar_tensor_tensor(
                        out=vt[:, par, half, j, :, 0:D],
                        in0=bv_b[:, half * P:(half + 1) * P].rearrange("p (h d) -> p h d", d=D),
                        scalar=mcol[:, par, j:j + 1],
                        in1=ps_j[:, slot, j * P:(j + 1) * P].rearrange("p (h d) -> p h d", d=D),
                        op0=ALU.mult, op1=ALU.add)
                ins.then_inc(emptied["v"], 1)

            def take_max(n, g2, job, slot):
                dve.wait_ge(job_done, job)
                wait(dve, max_in, (n - 1) * 32)
                link(dve.tensor_scalar(mt[:, g2, 0, :], ps_j[0:16, slot, 0:P], -1.0, None, ALU.mult))
                dve.scalar_tensor_tensor(out=mt[:, g2, 1, :], in0=ps_j[0:16, slot, 0:P], scalar=-1.0,
                                         in1=mt[:, g2, 0, :], op0=ALU.mult, op1=ALU.subtract
                                         ).then_inc(emptied["T"], 1)

            def maxima(b, hb, i):
                m = 4 * hb + i
                dve.wait_ge(s_done, b * 64 + (m + 1))
                col = 4 * (hb % 4) + i
                dve.tensor_reduce(mx[:, (hb // 4) % 2, col:col + 1], ps_s[:, m % 2, :], X,
                                  ALU.max).then_inc(mx_done, 1)

            def hot(b, c, job, quarter):
                if quarter == 0:
                    dve.wait_ge(idx_sem, (b + 1) * 16)
                    wait(dve, hot_rdy, b * 4 + c)
                    wait(dve, job_done, job)
                    dve.tensor_copy(idxf[:], idx_in[:, c * CH:(c + 1) * CH]).then_inc(idx_used, 1)
                    dve.wait_ge(idx_used, b * 4 + (c + 1))
                for j in range(4 * quarter, 4 * quarter + 4):
                    ins = dve.tensor_scalar(onehot[:, c % 2, j, :], idxf[:], float(j), None, ALU.is_equal)
                if quarter == 3:
                    ins.then_inc(hot_rdy, 1)

            def masked_inverse(b, par, half):
                u = b * 2 + half
                for p2 in range(2):
                    dve.wait_ge(gathered[p2], (u + 1) * GATHER)
                dve.wait_ge(tm_in, (b + 1) * 16)
                link(dve.reciprocal(rden[:, half, :], den[:, half, :]))
                wait(dve, bounce, (u - 1) * 16)
                dve.tensor_tensor(rden[:, half, :], rden[:, half, :], tm[:, par, :], ALU.mult
                                  ).then_inc(rden_rdy, 1)

            norm_stats(0)
            dve.wait_ge(small_in, 16)
            link(dve.tensor_scalar(lut_b[:, 1, :], lut_b[:, 0, :], -1.0, None, ALU.mult))
            link(dve.tensor_tensor(lut_b[:, 2, :], lut_b[:, 0, :], lut_b[:, 1, :], ALU.max))
            link(dve.tensor_reduce(lt[:, 0:1], lut_b[:, 2, :], X, ALU.max))
            link(dve.tensor_scalar(lt[:, 1:2].bitcast(U32), lt[:, 0:1].bitcast(U32), 0x7F800000, None,
                                   ALU.bitwise_and))
            link(dve.tensor_scalar(lt[:, 2:3], lt[:, 1:2], 2.0 ** -100, None, ALU.max))
            normalise(0, 0)
            link(dve.reciprocal(lt[:, 3:4], lt[:, 2:3]))
            link(dve.tensor_scalar(lt[:, 4:5], lt[:, 3:4], 2.0 ** 14, None, ALU.mult))
            link(dve.tensor_scalar(lut_b[:, 3, :], lut_b[:, 0, :], lt[:, 4:5], None, ALU.mult))
            link(dve.tensor_copy(lut16[:], lut_b[:, 3, :]))
            link(dve.tensor_tensor(lut_b[:, 4, :], lut_b[:, 3, :], lut16[:], ALU.subtract))
            link(dve.tensor_copy(lut_b[:, 3, :], lut16[:]))
            link(dve.tensor_scalar(scales[:, 0:1], lt[:, 2:3], 2.0 ** -25, None, ALU.mult))
            link(dve.tensor_scalar(scales[:, 1:2], lt[:, 3:4], 2.0 ** -30, None, ALU.mult))
            link(dve.tensor_scalar(lt[:, 5:6], lt[:, 2:3], lt[:, 2:3], None, ALU.mult))
            link(dve.tensor_scalar(lt[:, 6:7], lt[:, 5:6], lt[:, 2:3], None, ALU.mult))
            link(dve.tensor_scalar(scales[:, 2:3], lt[:, 6:7], 2.0 ** -9, None, ALU.mult))
            dve.wait_ge(ident_rdy, 2)
            link(dve.tensor_copy(ident16[:], ident[:]))
            for part in range(2):
                for j in range(LUT):
                    ins = dve.tensor_scalar(diag[:, part, j, :], ident16[:],
                                            lut_b[:, 3 + part, j:j + 1], None, ALU.mult)
            ins.then_inc(diag_rdy, 1)
            dve.wait_ge(const_in, 16 * 6)
            for half in range(2):
                take_q(0, 0, half, 3 * half + 1, (3 * half + 1) % 2)
                for stage in range(4):
                    cut(qp, stage)
                take_k(0, 0, half, 3 * half + 2, (3 * half + 2) % 2)
                for stage in range(4):
                    cut(kp, stage)
                take_v(0, 0, half, 3 * half + 3, (3 * half + 3) % 2)
            for h in range(AHEAD):
                for i in range(4):
                    maxima(0, h, i)
                if h == 3:
                    take_max(0, 0, 7, 1)
            for quarter in range(4):
                hot(0, 0, 0, quarter)
            Chain.base, Chain.per, Chain.k = Chain.k, LINKS, 0

            def body(b, par, load=True, last=False):
                order = jobs_of(last)
                Chain.b, Chain.k = b, 0
                last_of = {name: jobs_through(b, k) for k, (_, name) in enumerate(order)}
                for g in range(STEPS):
                    hb = g + AHEAD
                    for i in range(4):
                        if hb < H or not last:
                            maxima(b, hb, i)
                        for k, (gk, name) in enumerate(order):
                            if gk == g and name == "T" and i == 1:
                                take_max(b * 4 + (g // 4 + 1), (g // 4 + 1) % 2, jobs_through(b, k), k % 2)
                            if gk == g - 1 and name == "q":
                                cut(qp, i)
                            if gk == g - 1 and name == "k":
                                cut(kp, i)
                        if g == 0:
                            hot(b, 1, jobs_through(b, -1), i)
                        if g == 3:
                            hot(b, 2, last_of["L1"], i)
                        if g == 7:
                            hot(b, 3, last_of["L3"], i)
                        if g == 11 and not last:
                            hot(b + 1, 0, last_of["L5"], i)
                    for k, (gk, name) in enumerate(order):
                        if gk != g:
                            continue
                        job, half = jobs_through(b, k), g // 8
                        if name == "q":
                            take_q(b + 1, 1 - par, half, job, k % 2)
                        if name == "k":
                            take_k(b + 1, 1 - par, half, job, k % 2)
                        if name == "v":
                            take_v(b + 1, 1 - par, half, job, k % 2)
                    if g == 0 and not last:
                        norm_stats(b + 1)
                    if g == 2 and not last:
                        normalise(b + 1, jobs_through(b, -1))
                    if g == 6 and not (isinstance(b, int) and b == 0):
                        masked_inverse(b - 1, 1 - par, 1)
                    if g == 14:
                        masked_inverse(b, par, 0)
                if isinstance(b, int) and b == 0:
                    Chain.base -= LINKS - Chain.k

            batches(dve, body)
            Chain.base, Chain.b = Chain.base + LINKS * (B - 1) + Chain.k, 0
            Chain.k = 0
            masked_inverse(B - 1, 1, 1)

        @block.tensor
        def _(pe):
            def job_matmuls(b, name, g, slot):
                todo = []
                half = g // 8
                cols = slice(half * P, (half + 1) * P)
                if name in "qk":
                    w, src = (wq_sb, xn) if name == "q" else (wk_sb, cm)
                    for t in range(2):
                        todo.append((ps_j[:, slot, :], w[:, t, cols], src[:, t, :], t == 0, t == 1))
                if name == "v":
                    for j in range(4):
                        for t in range(2):
                            todo.append((ps_j[:, slot, j * P:(j + 1) * P], cm[:, t, j * P:(j + 1) * P],
                                         wv_sb[:, t, cols], t == 0, t == 1))
                if name[0] == "L":
                    c, part = int(name[1]) // 2, int(name[1]) % 2
                    for j in range(LUT):
                        todo.append((ps_j[:, slot, 0:CH], diag[:, part, j, :], onehot[:, c % 2, j, :],
                                     j == 0, j == LUT - 1))
                return todo

            def run(todo, count):
                for _ in range(min(count, len(todo))):
                    dst, lhs, rhs, start, stop = todo.pop(0)
                    ins = pe.matmul(dst, lhs, rhs, start=start, stop=stop)
                    if not todo:
                        ins.then_inc(job_done, 1)

            def scores_for_max(b, hb, i):
                half, h = (hb // 8) % 2, hb % 8
                m = 4 * hb + i
                wait(pe, mx_done, b * 64 + (m - 1))
                pe.matmul(ps_s[:, m % 2, :], qs[0:XROW, half, h, i * P:(i + 1) * P],
                          ks[0:XROW, half, h, :], start=True, stop=True).then_inc(s_done, 1)

            def turn_max(n2, slot):
                pe.transpose(ps_j[0:16, slot, 0:P], mx[:, n2, :], ident[:]).then_inc(job_done, 1)

            def before_job(b, k, last, name):
                kind, through = ordinal(b, k - 2, last)
                pe.wait_ge(emptied[kind], through)
                if name == "q":
                    pe.wait_ge(xn_rdy, b + 2)
                if name in "kv":
                    pe.wait_ge(cm_rdy, b + 2)
                if name[0] == "L":
                    pe.wait_ge(hot_rdy, b * 4 + (int(name[1]) // 2 + 1))

            pe.wait_ge(const_in, 16 * 6)
            pe.wait_ge(xn_rdy, 1)
            pe.wait_ge(cm_rdy, 1)
            for i, name in enumerate(FIRST[:6]):
                if i >= 2:
                    pe.wait_ge(emptied[FIRST[i - 2]], FIRST[:i - 1].count(FIRST[i - 2]))
                run(job_matmuls(0, name, 8 * (i // 3), (i + 1) % 2), 99)
            pe.wait_ge(mem_rdy, 1)
            pe.wait_ge(diag_rdy, 1)
            pe.wait_ge(stack_in[0], NSTACK)
            for h in range(AHEAD):
                for i in range(4):
                    scores_for_max(0, h, i)
                if h == 3:
                    pe.wait_ge(mx_done, 16)
                    pe.wait_ge(emptied["k"], 2)
                    turn_max(0, 1)

            def body(b, par, load=True, last=False):
                order = jobs_of(last)
                for g in range(STEPS):
                    s, j = g // 4, g % 4
                    half, h0 = s // 2, 4 * (s % 2)
                    hb = g + AHEAD
                    more = hb < H or not last
                    if hb == 8:
                        pe.wait_ge(stack_in[1], (b + 1) * NSTACK)
                    if hb == 16 and more:
                        pe.wait_ge(stack_in[0], (b + 2) * NSTACK)
                    if j == 0:
                        pe.wait_ge(max_in, (b * 4 + (s + 1)) * 32)
                    todo, mine = [], [(k, name) for k, (gk, name) in enumerate(order) if gk == g]
                    for i in range(4):
                        m = 4 * g + i
                        wait(pe, exp_done, b * 64 + (m - 1))
                        pe.matmul(ps_t[:, m % 2, :], ks[0:SROWS, half, h0 + i, j * P:(j + 1) * P],
                                  qs[0:SROWS, half, h0 + i, :], start=True, stop=True).then_inc(t_done, 1)
                        if more:
                            scores_for_max(b, hb, i)
                        for k, name in mine:
                            if name == "T":
                                if i == 1:
                                    before_job(b, k, last, name)
                                    pe.wait_ge(mx_done, (b * 4 + (s + 2)) * 16)
                                    turn_max((s + 1) % 2, k % 2)
                            else:
                                first = 1 if len(mine) > 1 else 0
                                if i == first:
                                    before_job(b, k, last, name)
                                    todo = job_matmuls(b, name, g, k % 2)
                                    each = -(-len(todo) // (4 - first))
                                if i >= first:
                                    run(todo, each)
                    pe.wait_ge(exp_done, b * 64 + (4 * g + 4))
                    if j == 0:
                        wait(pe, o_rdy, b * 4 + (s - 1))
                    if g % 8 == 0:
                        pe.wait_ge(emptied["v"], b * 2 + (half + 1))
                    for i in range(4):
                        ins = pe.matmul(ps_o[32 * i:32 * i + DW, s % 2, :], vt[:, par, half, j, h0 + i, :],
                                        probs[:, g % 2, i, :], start=(j == 0), stop=(j == 3))
                    ins.then_inc(pv_done, 1)

            batches(pe, body)


GATHER = 16 * 5
LINKS = 2 + 2 * 2 * 3 + 4 + 2


def ffn(nc, st, xmid, out, w_hi, w_lo, scales, ident16):
    def sb(name, shape, dt=F32):
        return st.enter_context(nc.sbuf_tensor(name, shape, dt))

    def sem(name):
        return st.enter_context(nc.semaphore(name))

    NG = B * C // GT
    xg = sb("xg", [P, 2, GTT, T])
    xs = sb("xs", [P, 2, T])
    xh = sb("xh", [P, GTT, 2, T], F16)
    xt = sb("xt", [P, 2, 2, KT, GT], F16)
    sil = sb("sil", [P, 2, GT])
    hf = sb("hf", [P, 2, GT])
    ht = sb("ht", [P, IT, 2, GT], F16)
    res = sb("res", [P, 2, T])
    stats = sb("f_stats", [P, GTT, 6])
    mv = sb("f_mv", [P, GTT, 2])
    ve = sb("f_ve", [P, GTT])
    mhalf = sb("f_mhalf", [P, GTT])
    rstd = sb("f_rstd", [P, GTT])
    ps_g = st.enter_context(nc.psum_tensor("ps_g", [P, 2, 512], F32))
    ps_u = st.enter_context(nc.psum_tensor("ps_u", [P, 2, 512], F32))
    ps_d = st.enter_context(nc.psum_tensor("ps_d", [P, 2, 512], F32))
    ps_x = st.enter_context(nc.psum_tensor("ps_x", [P, 2, 1024], F16))

    settled = sem("f_settled")
    x_sem = sem("f_x_in")
    half_rdy = sem("f_half_rdy")
    var_rdy = sem("f_var_rdy")
    rstd_rdy = sem("f_rstd_rdy")
    xs_rdy = sem("f_xs_rdy")
    fdv = sem("f_dv")
    xh_rdy = sem("f_xh_rdy")
    turned = sem("f_turned")
    xt_rdy = sem("f_xt_rdy")
    gate_done = sem("f_gate_done")
    up_done = sem("f_up_done")
    sil_rdy = sem("f_sil_rdy")
    h_rdy = sem("f_h_rdy")
    ht_rdy = sem("f_ht_rdy")
    down_done = sem("f_down_done")
    res_rdy = sem("f_res_rdy")
    stored = [sem("f_stored0"), sem("f_stored1")]

    def width(i):
        return P if i < IT - 1 else ILAST

    def groups(eng, body):
        body(0, 0)
        body(1, 1)
        with eng.Fori(1, NG // 2 - 1) as pair:
            body(pair * 2, 0)
            body(pair * 2 + 1, 1)
        body(NG - 2, 0)
        body(NG - 1, 1, last=True)

    per_group = GT // C
    rows = lambda a, n: a[bass.ds(n * per_group, per_group), :, :].rearrange("b (t p) f -> p (b t) f", p=P)

    with nc.Block() as block:

        @block.sync
        def _(sp):
            sp.dma_start(xg[:, 0, :, :], rows(xmid, 0)).then_inc(x_sem, 16)

            def body(n, par, last=False):
                if not last:
                    wait(sp, res_rdy, n * GTT)
                    settle(sp, settled)
                    sp.wait_ge(xs_rdy, (n + 1) * GTT)
                    settle(sp, settled)
                    sp.dma_start(xg[:, 1 - par, :, :], rows(xmid, n + 1)).then_inc(x_sem, 16)
                for t in range(GTT):
                    sp.wait_ge(res_rdy, n * GTT + (t + 1))
                    settle(sp, settled)
                    b, r = n * per_group + t // 2, (t % 2) * P
                    sp.dma_start(out[bass.ds(b, 1), r:r + P, :].rearrange("o p f -> (o p) f"),
                                 res[:, t % 2, :]).then_inc(stored[t % 2], 16)

            groups(sp, body)
            for q in stored:
                sp.wait_ge(q, 16 * NG * GTT // 2)

        @block.gpsimd
        def _(pool):
            pool.memset(mhalf[:], -0.5).then_inc(half_rdy, 1)
            pool.wait_ge(half_rdy, 1)

            def inv_std(n):
                pool.wait_ge(var_rdy, n + 1)
                pool.tensor_tensor(rstd[:], ve[:], mhalf[:], ALU.pow).then_inc(rstd_rdy, 1)

            inv_std(0)

            def body(n, par, last=False):
                if not last:
                    inv_std(n + 1)

            groups(pool, body)

        @block.scalar
        def _(act):
            def take_turned(n, par):
                for t in range(GTT):
                    act.wait_ge(turned, n * GTT + (t + 1))
                    act.activation(xt[:, par, :, :, t * P:(t + 1) * P],
                                   ps_x[:, t % 2, :].rearrange("p (a k t) -> p a k t", a=2, k=KT),
                                   ACT.Copy).then_inc(xt_rdy, 1)

            take_turned(0, 0)

            def body(n, par, last=False):
                for i in range(IT):
                    w = width(i)
                    act.wait_ge(gate_done, n * IT + (i + 1))
                    wait(act, h_rdy, n * IT + (i - 1))
                    act.activation(sil[0:w, i % 2, :], ps_g[0:w, i % 2, :], ACT.Silu,
                                   scale=scales[0:w, 0:1]).then_inc(sil_rdy, 1)
                if not last:
                    take_turned(n + 1, 1 - par)

            groups(act, body)

        @block.vector
        def _(dve):
            def norm(n, par):
                dve.wait_ge(x_sem, (n + 1) * 16)
                for t in range(GTT):
                    ins = dve.bn_stats(stats[:, t, :], xg[:, par, t, :])
                ins.then_inc(fdv, 1)
                dve.wait_ge(fdv, n * 2 + 1)
                settle(dve, settled)
                for t in range(GTT):
                    ins = dve.bn_aggr(mv[:, t, :], stats[:, t, :])
                ins.then_inc(fdv, 1)
                dve.wait_ge(fdv, n * 2 + 2)
                dve.tensor_scalar(ve[:], mv[:, :, 1], EPS, 2.0 ** -22, ALU.add, ALU.mult).then_inc(var_rdy, 1)

            def parts(n, par):
                dve.wait_ge(rstd_rdy, n + 1)
                wait(dve, turned, n * GTT)
                for t in range(GTT):
                    dve.tensor_scalar(xs[:, t % 2, :], xg[:, par, t, :], mv[:, t, 0:1], rstd[:, t:t + 1],
                                      ALU.subtract, ALU.mult).then_inc(xs_rdy, 1)
                    dve.wait_ge(xs_rdy, n * GTT + (t + 1))
                    dve.tensor_copy(xh[:, t, 0, :], xs[:, t % 2, :]).then_inc(xh_rdy, 1)
                    dve.wait_ge(xh_rdy, (n * GTT + t) * 2 + 1)
                    dve.tensor_tensor(xh[:, t, 1, :], xs[:, t % 2, :], xh[:, t, 0, :], ALU.subtract
                                      ).then_inc(xh_rdy, 1)

            norm(0, 0)
            parts(0, 0)

            def body(n, par, last=False):
                for i in range(IT):
                    w = width(i)
                    dve.wait_ge(sil_rdy, n * IT + (i + 1))
                    dve.wait_ge(up_done, n * IT + (i + 1))
                    if i == 0:
                        wait(dve, down_done, n * GTT)
                    dve.scalar_tensor_tensor(out=hf[0:w, i % 2, :], in0=sil[0:w, i % 2, :],
                                             scalar=scales[0:w, 1:2], in1=ps_u[0:w, i % 2, :],
                                             op0=ALU.mult, op1=ALU.mult).then_inc(h_rdy, 1)
                    dve.wait_ge(h_rdy, n * IT + (i + 1))
                    dve.tensor_copy(ht[0:w, i, 0, :], hf[0:w, i % 2, :]).then_inc(ht_rdy, 1)
                    dve.wait_ge(ht_rdy, (n * IT + i) * 2 + 1)
                    dve.tensor_tensor(ht[0:w, i, 1, :], hf[0:w, i % 2, :], ht[0:w, i, 0, :], ALU.subtract
                                      ).then_inc(ht_rdy, 1)
                    if i == 6 and not last:
                        norm(n + 1, 1 - par)
                    if i == 7 and not last:
                        parts(n + 1, 1 - par)
                for t in range(GTT):
                    dve.wait_ge(down_done, n * GTT + (t + 1))
                    wait(dve, stored[t % 2], (n * 2 + t // 2) * 16)
                    dve.scalar_tensor_tensor(out=res[:, t % 2, :], in0=ps_d[:, t % 2, :],
                                             scalar=scales[:, 2:3], in1=xg[:, par, t, :],
                                             op0=ALU.mult, op1=ALU.add).then_inc(res_rdy, 1)

            groups(dve, body)

        @block.tensor
        def _(pe):
            def turn(n, par):
                for t in range(GTT):
                    pe.wait_ge(xh_rdy, (n * GTT + (t + 1)) * 2)
                    wait(pe, xt_rdy, n * GTT + (t - 1))
                    for part in range(2):
                        for k in range(KT):
                            c = (part * KT + k) * P
                            ins = pe.transpose(ps_x[:, t % 2, c:c + P], xh[:, t, part, k * P:(k + 1) * P],
                                               ident16[:])
                    ins.then_inc(turned, 1)

            turn(0, 0)

            def body(n, par, last=False):
                pe.wait_ge(xt_rdy, (n + 1) * GTT)
                for i in range(IT):
                    w = width(i)
                    for base, ps, done, free in ((GATE0, ps_g, gate_done, sil_rdy), (UP0, ps_u, up_done, h_rdy)):
                        wait(pe, free, n * IT + (i - 1))
                        for k in range(KT):
                            c = base + k * INTER + i * P
                            for wp, part in ((w_hi, 0), (w_hi, 1), (w_lo, 0)):
                                first, end = k == 0 and wp is w_hi and part == 0, k == KT - 1 and wp is w_lo
                                ins = pe.matmul(ps[0:w, i % 2, :], wp[:, c:c + w], xt[:, par, part, k, :],
                                                start=first, stop=end)
                        ins.then_inc(done, 1)
                if not last:
                    turn(n + 1, 1 - par)
                pe.wait_ge(ht_rdy, (n + 1) * (2 * IT))
                for t in range(GTT):
                    wait(pe, res_rdy, n * GTT + (t - 1))
                    for i in range(IT):
                        w = width(i)
                        c = DOWN0 + i * T
                        for wp, part in ((w_hi, 0), (w_lo, 0), (w_hi, 1)):
                            ins = pe.matmul(ps_d[:, t % 2, :], ht[0:w, i, part, t * P:(t + 1) * P],
                                            wp[0:w, c:c + T], start=(i == 0 and wp is w_hi and part == 0),
                                            stop=(i == IT - 1 and part == 1))
                    ins.then_inc(down_done, 1)

            groups(pe, body)


def kernel(x, ctx_2048, mask_Bx1x2048_fk1, L0_xattn_Wq, L0_xattn_bq, L0_xattn_Wk, L0_xattn_bk, L0_xattn_Wv,
           L0_xattn_bv, L0_ffn_lut, L0_ffn_gate_idx, L0_ffn_up_idx, L0_ffn_down_idx):
    import numpy as np
    import concourse.bacc as bacc
    from concourse.bass_utils import run_bass_kernel_spmd

    c = np.ascontiguousarray
    a = lambda v: np.asarray(v)

    def tiles(i):
        t = a(i).T
        pad = -t.shape[0] % P
        t = np.pad(t, ((0, pad), (0, 0)))
        return t.reshape(-1, P, t.shape[1]).transpose(1, 0, 2).reshape(P, -1)

    def by_row(v):
        v = a(v)
        return v.reshape(2, H // 2, D, -1).transpose(0, 2, 1, 3).reshape(v.shape)

    idx = np.concatenate([tiles(L0_ffn_gate_idx), tiles(L0_ffn_up_idx), tiles(L0_ffn_down_idx)], axis=1)
    arrays = {
        "x": a(x), "ctx": a(ctx_2048), "mask": a(mask_Bx1x2048_fk1),
        "wq": c(by_row(L0_xattn_Wq).T), "bq": c(by_row(L0_xattn_bq).reshape(2, P).T),
        "wk": c(by_row(L0_xattn_Wk).T), "bk": c(by_row(L0_xattn_bk).reshape(2, P).T),
        "wv": c(a(L0_xattn_Wv).T), "bv": c(a(L0_xattn_bv).reshape(1, C)),
        "lut": c(a(L0_ffn_lut).reshape(1, LUT)), "idx": c(idx.reshape(P, B, WB)),
    }
    nc = bacc.Bacc("TRN2", target_bir_lowering=False, num_devices=1)
    args = [nc.dram_tensor(n, v.shape, mybir.dt.from_np(v.dtype), kind="ExternalInput").ap()
            for n, v in arrays.items()]
    out = nc.dram_tensor("out", [B, C, T], F32, kind="ExternalOutput").ap()
    build(nc, *args, out)
    r = run_bass_kernel_spmd(nc, [arrays], core_ids=[0])
    return r.results[0]["out"]
```

```python
from contextlib import ExitStack

import concourse.bass as bass
from concourse import mybir

ALU = mybir.AluOpType
ACT = mybir.ActivationFunctionType
X = mybir.AxisListType.X
F32 = mybir.dt.float32
F16 = mybir.dt.float16
BF16 = mybir.dt.bfloat16
I32 = mybir.dt.int32
U32 = mybir.dt.uint32

P = 128
B, C, T = 16, 256, 512
H, D = 16, 16
INTER, LUT = 1376, 16
KT = T // P
IT = -(-INTER // P)
ILAST = INTER - (IT - 1) * P
GATE0, UP0, DOWN0 = 0, KT * INTER, 2 * KT * INTER
WCOLS = DOWN0 + IT * T
WB = WCOLS // B
CH = WB // 4
Q = 32
LQ = LUT // 4
NEG = 1.0e6
EPS = 1e-5
SLOTS = 6
QPART = (0, 0, 1, 0, 2, 1)
KPART = (0, 1, 0, 2, 0, 1)
MROW = SLOTS * D
XROW = MROW + SLOTS
SROWS = XROW + 2
DW = D + 1
GT = 512
GTT = GT // P

JOBS = {0: ["L0"], 1: ["L1"], 2: ["L2"], 3: ["T", "v"], 4: ["q"], 5: ["k"], 6: ["L3"], 7: ["T"],
        8: ["L4"], 9: ["L5"], 10: ["L6"], 11: ["T", "v"], 12: ["q"], 13: ["k"], 14: ["L7"], 15: ["T"]}
SBANKS = 3
STEPS = 16
ORDER = [(g, name) for g in range(STEPS) for name in JOBS[g]]
LAST_ORDER = [(g, name) for g, name in ORDER if name[0] == "L" or (name == "T" and g < 15)]
NJ = len(ORDER)
AHEAD = 5
FIRST = ["q", "k", "v", "q", "k", "v", "T"]
PER = {c: sum(name[0] == c for _, name in ORDER) for c in "LqkvT"}


def max_bank(m):
    return m % (4 * H) % SBANKS


def max_bank_before(m):
    return next(k for k in range(m - 1, -99, -1) if max_bank(k) == max_bank(m))


def wait(eng, sem, value):
    if not (isinstance(value, int) and value <= 0):
        eng.wait_ge(sem, value)


def settle(eng, sem):
    eng.sem_inc(sem, 1)


def batches(eng, body):
    body(0, 0)
    body(1, 1)
    with eng.Fori(1, B // 2 - 1) as pair:
        body(pair * 2, 0)
        body(pair * 2 + 1, 1)
    body(B - 2, 0, load=False)
    body(B - 1, 1, load=False, last=True)


def jobs_of(last):
    return LAST_ORDER if last else ORDER


def ordinal(b, k, last=False):
    if k < 0 and isinstance(b, int) and b == 0:
        return FIRST[k], FIRST[:len(FIRST) + k + 1].count(FIRST[k])
    order, back = (ORDER, b - 1) if k < 0 else (jobs_of(last), b)
    kind = order[k][1][0]
    here = sum(name[0] == kind for _, name in order[:k % len(order) + 1])
    return kind, FIRST.count(kind) + PER[kind] * back + here


def build(nc, x, ctx, mask, wq, bq, wk, bk, wv, bv, lut, idx, out):
    xmid = nc.dram_tensor("xmid", [B, C, T], F32, kind="Internal").ap()
    mask_rows = nc.dram_tensor("mask_rows", [B, 2, SLOTS, T], BF16, kind="Internal").ap()
    den_rows = nc.dram_tensor("den_rows", [2, H // 2, T], F32, kind="Internal").ap()
    with ExitStack() as keep:
        w_hi = keep.enter_context(nc.sbuf_tensor("w_hi", [P, WCOLS], F16))
        w_lo = keep.enter_context(nc.sbuf_tensor("w_lo", [P, WCOLS], F16))
        scales = keep.enter_context(nc.sbuf_tensor("scales", [P, 4], F32))
        ident16 = keep.enter_context(nc.sbuf_tensor("ident16", [P, P], F16))
        with ExitStack() as st:
            attention(nc, st, x, ctx, mask, wq, bq, wk, bk, wv, bv, lut, idx, xmid, mask_rows, den_rows,
                      w_hi, w_lo, scales, ident16)
        with ExitStack() as st:
            ffn(nc, st, xmid, out, w_hi, w_lo, scales, ident16)


def attention(nc, st, x, ctx, mask, wq, bq, wk, bk, wv, bv, lut, idx, xmid, mask_rows, den_rows,
              w_hi, w_lo, scales, ident16):
    def sb(name, shape, dt=F32):
        return st.enter_context(nc.sbuf_tensor(name, shape, dt))

    def sem(name):
        return st.enter_context(nc.semaphore(name))

    qs = sb("qs", [P, 2, 8, T], BF16)
    ks = sb("ks", [P, 2, 8, T], BF16)
    vt = sb("vt", [P, 2, 2, 4, 8, DW])
    probs = sb("probs", [P, 2, 4, T])
    x_in = sb("x_in", [P, 2, T])
    c_in = sb("c_in", [P, 2, T])
    xn = sb("xn", [P, 2, T])
    cm = sb("cm", [P, 2, T])
    mb = sb("mb", [P, 2, T])
    mcol = sb("mcol", [P, 2, 4])
    full = sb("full", [P, T])
    rest = sb("rest", [P, T])
    qp = sb("qp", [P, 3, T], BF16)
    kp = sb("kp", [P, 3, T], BF16)
    o_sb = sb("o_sb", [P, 2, T])
    num = sb("num", [P, 2, T])
    rb = sb("rb", [P, T])
    xr = sb("xr", [P, T])
    den = sb("den", [64, 2, 64])
    rden = sb("rden", [64, 2, 64])
    tm = sb("tm", [64, 2, 64])
    idx_in = sb("idx_in", [P, 4, CH], I32)
    idxf = sb("idxf", [P, 2, 4, CH], F16)
    onehot = sb("onehot", [P, 2, LQ, 4, CH], F16)
    diag = sb("diag", [P, 2, LQ, Q], F16)
    eye = sb("eye", [P, 3, Q])
    entry = sb("entry", [P, LQ])
    lut_q = sb("lut_q", [P, 3, LQ])
    ident = sb("ident", [P, P])
    wq_sb = sb("wq_sb", [P, 2, C])
    wk_sb = sb("wk_sb", [P, 2, C])
    wv_sb = sb("wv_sb", [P, 2, C])
    b_sb = sb("b_sb", [P, 4])
    bv_b = sb("bv_b", [P, C])
    lut_b = sb("lut_b", [P, 3, LUT])
    lut16 = sb("lut16", [P, LQ], F16)
    lt = sb("lt", [P, 8])
    stats = sb("stats", [P, 2, 6])
    mv = sb("mv", [P, 2, 2])
    ve = sb("ve", [P, 2])
    mhalf = sb("mhalf", [P, 2])
    rstd = sb("rstd", [P, 2])
    mx = sb("mx", [P, 2, 16])
    mt = sb("mt", [16, 2, 2, P], BF16)

    ps_s = st.enter_context(nc.psum_tensor("ps_s", [P, SBANKS, 512], F32))
    ps_t = st.enter_context(nc.psum_tensor("ps_t", [P, 2, 512], F32))
    ps_o = st.enter_context(nc.psum_tensor("ps_o", [P, 512], F32))
    ps_j = st.enter_context(nc.psum_tensor("ps_j", [P, 2, 512], F32))

    settled = sem("settled")
    const_in = sem("const_in")
    small_in = sem("small_in")
    mask_in = sem("mask_in")
    mrow_out = sem("mrow_out")
    mparts_rdy = sem("mparts_rdy")
    ident_rdy = sem("ident_rdy")
    half_rdy = sem("half_rdy")
    mem_rdy = sem("mem_rdy")
    diag_rdy = sem("diag_rdy")
    dv = sem("dv")
    inp = sem("inp")
    idx_sem = sem("idx_sem")
    idxf_rdy = sem("idxf_rdy")
    var_rdy = sem("var_rdy")
    rstd_rdy = sem("rstd_rdy")
    xn_rdy = sem("xn_rdy")
    cm_rdy = sem("cm_rdy")
    rounded = sem("rounded")
    rest_rdy = sem("rest_rdy")
    parts_rdy = sem("parts_rdy")
    stack_in = [sem("stack_in0"), sem("stack_in1")]
    mask_set = [sem("mask_set0"), sem("mask_set1")]
    s_done = sem("s_done")
    mx_done = sem("mx_done")
    t_done = sem("t_done")
    exp_done = sem("exp_done")
    pv_done = sem("pv_done")
    job_done = sem("job_done")
    emptied = {"q": sem("q_out"), "k": sem("k_out"), "v": sem("v_out"), "T": sem("max_out"), "L": sem("w_out")}
    max_in = sem("max_in")
    hot_rdy = sem("hot_rdy")
    o_rdy = sem("o_rdy")
    gathered = [sem("gathered0"), sem("gathered1")]
    tm_in = sem("tm_in")
    den_sem = sem("den_sem")
    rden_rdy = sem("rden_rdy")
    bounce = sem("bounce")
    rb_in = sem("rb_in")
    res_rdy = sem("res_rdy")
    sum_rdy = sem("sum_rdy")
    stored = sem("stored")

    NSTACK = 16 * 2 * SLOTS

    def jobs_through(b, k):
        return len(FIRST) + NJ * b + k + 1

    def spread_mask(eng, b, half):
        for side, dst in ((0, qs), (1, ks)):
            rows = mask_rows[bass.ds(b, 1), side, :, :].rearrange("o s t -> (o s) t")
            eng.dma_start(dst[MROW:XROW, half, :, :],
                          rows.unsqueeze(1).to_broadcast([SLOTS, 8, T])).then_inc(mask_set[half], 16)

    with nc.Block() as block:

        @block.sync
        def _(sp):
            def load_inputs(b, par):
                sp.dma_start(x_in[:], x[bass.ds(b, 1), :, :].rearrange("o (t p) f -> p (o t) f", p=P)).then_inc(inp, 16)
                sp.dma_start(c_in[:], ctx[bass.ds(b, 1), :, :].rearrange("o (t p) f -> p (o t) f", p=P)).then_inc(inp, 16)
                sp.dma_start(mb[:, par, :], mask[bass.ds(b, 1), 0, :].to_broadcast([P, T])).then_inc(inp, 16)
                with nc.allow_non_contiguous_dma("512 mask values, positions to the partitions"):
                    sp.dma_start(mcol[:, par, :], mask[bass.ds(b, 1), 0, :].rearrange("o (j p) -> p (o j)", p=P)
                                 ).then_inc(inp, 16)

            def stack(b, half, readers):
                sp.wait_ge(parts_rdy, b * 4 + 2 * half + 2)
                settle(sp, settled)
                wait(sp, t_done, readers)
                for slot in range(SLOTS):
                    for dst, src, part in ((qs, qp, QPART[slot]), (ks, kp, KPART[slot])):
                        sp.dma_start(dst[slot * D:(slot + 1) * D, half, :, :],
                                     src[:, part, :]).then_inc(stack_in[half], 16)

            def gather(b, s):
                if isinstance(b, int) and 4 * b + s == 0:
                    return
                half, g2 = ((s - 1) % 4) // 2, (s - 1) % 2
                sp.wait_ge(o_rdy, b * 4 + s)
                settle(sp, settled)
                wait(sp, res_rdy, b * 2 + (-2, -1, -1, 0)[s])
                for i in range(4):
                    sp.dma_start(num[64 * g2 + 16 * i:64 * g2 + 16 * i + 16, half, :],
                                 o_sb[32 * i:32 * i + 16, g2, :]).then_inc(gathered[g2], 16)
                sp.dma_start(den[32 * g2:32 * g2 + 32, half, :], o_sb[D:P:32, g2, :]).then_inc(gathered[g2], 16)

            def max_rows(n, half, g2):
                sp.wait_ge(emptied["T"], n + 1)
                for part in range(2):
                    sp.dma_start(qs[XROW + part:XROW + part + 1, half, 4 * g2:4 * g2 + 4, :],
                                 mt[:, g2, part, :]).then_inc(max_in, 16)

            sp.dma_start(num[0:B, 0, :], mask.rearrange("b o t -> b (o t)")).then_inc(mask_in, 16)
            load_inputs(0, 0)
            for dst, src in ((wq_sb, wq), (wk_sb, wk), (wv_sb, wv)):
                sp.dma_start(dst[:], src.rearrange("(k p) o -> p k o", p=P)).then_inc(const_in, 16)
            sp.dma_start(b_sb[:, 0:2], bq).then_inc(const_in, 16)
            sp.dma_start(b_sb[:, 2:4], bk).then_inc(const_in, 16)
            sp.dma_start(bv_b[:], bv.to_broadcast([P, C])).then_inc(const_in, 16)
            sp.dma_start(lut_b[:, 0, :], lut.to_broadcast([P, LUT])).then_inc(small_in, 16)
            with nc.allow_non_contiguous_dma("every fourth entry of the table"):
                for a in range(4):
                    sp.dma_start(lut_q[Q * a:Q * a + Q, 0, :], lut[:, a:LUT:4].to_broadcast([Q, LQ])
                                 ).then_inc(small_in, 16)
            for side in range(2):
                sp.wait_ge(mparts_rdy, side + 1)
                for slot in range(SLOTS):
                    part = (QPART, KPART)[side][slot]
                    src = o_sb[0:B, side, :] if part < 2 else xr[0:B, :]
                    at = part if part < 2 else side
                    sp.dma_start(mask_rows[:, side, slot, :],
                                 src.bitcast(BF16)[:, at * T:(at + 1) * T]).then_inc(mrow_out, 16)
            sp.wait_ge(mem_rdy, 1)
            sp.wait_ge(mrow_out, 2 * 16 * SLOTS)
            stack(0, 0, 0)
            sp.wait_ge(xn_rdy, 1)
            sp.wait_ge(cm_rdy, 1)
            load_inputs(1, 1)
            max_rows(0, 0, 0)

            def body(b, par, load=True, last=False):
                stack(b, 1, b * 64)
                gather(b, 0)
                max_rows(b * 4 + 1, 0, 1)
                gather(b, 1)
                max_rows(b * 4 + 2, 1, 0)
                if load:
                    sp.wait_ge(xn_rdy, b + 2)
                    settle(sp, settled)
                    sp.wait_ge(cm_rdy, b + 2)
                    settle(sp, settled)
                    sp.wait_ge(emptied["v"], b * 2 + 2)
                    settle(sp, settled)
                    sp.wait_ge(emptied["k"], b * 2 + 2)
                    settle(sp, settled)
                    load_inputs(b + 2, par)
                if not last:
                    stack(b + 1, 0, b * 64 + 32)
                gather(b, 2)
                max_rows(b * 4 + 3, 1, 1)
                gather(b, 3)
                if not last:
                    max_rows(b * 4 + 4, 0, 0)

            batches(sp, body)
            gather(B, 0)

        @block.gpsimd
        def _(pool):
            pool.memset(ident[:], 0.0).then_inc(ident_rdy, 1)
            pool.wait_ge(ident_rdy, 1)
            pool.affine_select(out=ident[:], in_=ident[:], compare_op=ALU.not_equal, fill=1.0, base=0,
                               pattern=[[-1, P]], channel_multiplier=1).then_inc(ident_rdy, 1)

            def mask_context(b, par, jobs):
                pool.wait_ge(inp, (b + 1) * 64)
                wait(pool, job_done, jobs)
                for t in range(2):
                    ins = pool.tensor_tensor(cm[:, t, :], c_in[:, t, :], mb[:, par, :], ALU.mult)
                ins.then_inc(cm_rdy, 1)

            def inv_std(b):
                pool.wait_ge(var_rdy, b + 1)
                pool.tensor_tensor(rstd[:], ve[:], mhalf[:], ALU.pow).then_inc(rstd_rdy, 1)

            def load_indices(b, c):
                pool.dma_start(idx_in[:], idx[bass.ds(b, 1), c, :, :, :].rearrange("o p g n -> p (o g) n")
                               ).then_inc(idx_sem, 16)

            def cast_indices(b, c, load=True):
                pool.wait_ge(idx_sem, (b * 4 + (c + 1)) * 16)
                wait(pool, hot_rdy, b * 4 + (c - 1))
                settle(pool, settled)
                pool.tensor_copy(idxf[:, c % 2, :, :], idx_in[:]).then_inc(idxf_rdy, 1)
                if load:
                    pool.wait_ge(idxf_rdy, b * 4 + (c + 1))
                    settle(pool, settled)
                    load_indices(b + (c + 1) // 4, (c + 1) % 4)

            load_indices(0, 0)
            pool.wait_ge(half_rdy, 1)
            mask_context(0, 0, 0)
            inv_std(0)
            pool.wait_ge(mrow_out, 2 * 16 * SLOTS)
            pool.wait_ge(mem_rdy, 1)
            spread_mask(pool, 0, 0)
            for c in range(3):
                cast_indices(0, c)

            def finish(b, half):
                u = b * 2 + half
                pool.wait_ge(rden_rdy, u + 1)
                settle(pool, settled)
                pool.dma_start(den_rows[half, :, :].rearrange("h (c t) -> (h c) t", t=64),
                               rden[:, half, :]).then_inc(bounce, 16)
                wait(pool, stored, u * 16)
                settle(pool, settled)
                pool.dma_start(xr[:], x[bass.ds(b, 1), half * P:(half + 1) * P, :]
                               .rearrange("o p f -> (o p) f")).then_inc(rb_in, 16)
                pool.wait_ge(bounce, (u + 1) * 16)
                settle(pool, settled)
                pool.dma_start(rb[:], den_rows[half, :, :].unsqueeze(1).to_broadcast([8, D, T])
                               ).then_inc(rb_in, 16)
                pool.wait_ge(rb_in, (u + 1) * 32)
                for p2 in range(2):
                    pool.wait_ge(gathered[p2], (u + 1) * GATHER)
                pool.tensor_tensor(rb[:], num[:, half, :], rb[:], ALU.mult).then_inc(res_rdy, 1)
                pool.wait_ge(res_rdy, u + 1)
                pool.tensor_tensor(xr[:], xr[:], rb[:], ALU.add).then_inc(sum_rdy, 1)
                pool.wait_ge(sum_rdy, u + 1)
                settle(pool, settled)
                pool.dma_start(xmid[bass.ds(b, 1), half * P:(half + 1) * P, :].rearrange("o p f -> (o p) f"),
                               xr[:]).then_inc(stored, 16)

            def load_tm(b, par):
                m8 = mask[bass.ds(b, 1), 0, :].rearrange("o (c t) -> o c t", t=64)
                pool.dma_start(tm[:, par, :], m8.to_broadcast([8, 8, 64])).then_inc(tm_in, 16)

            def body(b, par, load=True, last=False):
                wait(pool, t_done, b * 64)
                settle(pool, settled)
                spread_mask(pool, b, 1)
                if not last:
                    mask_context(b + 1, 1 - par, jobs_through(b, -1))
                    inv_std(b + 1)
                cast_indices(b, 3, load=not last)
                load_tm(b, par)
                if not last:
                    cast_indices(b + 1, 0)
                if not (isinstance(b, int) and b == 0):
                    finish(b - 1, 1)
                if not last:
                    pool.wait_ge(t_done, b * 64 + 32)
                    settle(pool, settled)
                    spread_mask(pool, b + 1, 0)
                    for c in range(1, 3):
                        cast_indices(b + 1, c)
                finish(b, 0)

            batches(pool, body)
            finish(B - 1, 1)
            pool.wait_ge(stored, 16 * 2 * B)

        @block.scalar
        def _(act):
            def round_part(b, half, which, part):
                parts = (qp, kp)[which]
                if part == 0:
                    act.wait_ge(emptied["qk"[which]], b * 2 + (half + 1))
                    if half == 0:
                        wait(act, stack_in[1], b * NSTACK)
                    else:
                        act.wait_ge(stack_in[0], (b + 1) * NSTACK)
                else:
                    act.wait_ge(rest_rdy, b * 4 + (2 * half + which + 1))
                act.activation(parts[:, part, :], (full, rest)[part][:], ACT.Copy).then_inc(rounded, 1)

            def take_out(n, p2, before):
                act.wait_ge(pv_done, n * 4 + 4)
                wait(act, gathered[p2], before * GATHER)
                act.activation(o_sb[:, p2, :], ps_o[:], ACT.Copy).then_inc(o_rdy, 1)

            for half in range(2):
                for which in range(2):
                    for part in range(2):
                        round_part(0, half, which, part)

            def body(b, par, load=True, last=False):
                order = jobs_of(last)
                for g in range(STEPS):
                    for i in range(4):
                        s = g // 4
                        if g % 4 == 0 and i == 0 and not (isinstance(b, int) and b == 0 and s == 0):
                            take_out(b * 4 + (s - 1), (s - 1) % 2, b * 2 + (-1, 0, 0, 1)[s])
                        m = 4 * g + i
                        act.wait_ge(t_done, b * 64 + (m + 1))
                        if i == 0:
                            wait(act, pv_done, b * 16 + (g - 1))
                        act.activation(probs[:, g % 2, i, :], ps_t[:, m % 2, :], ACT.Exp,
                                       scale=0.25).then_inc(exp_done, 1)
                        for gk, name in order:
                            if gk == g - 1 and name in "qk" and i % 2 == 0:
                                round_part(b + 1, g // 8, "qk".index(name), i // 2)
                    for k, (gk, name) in enumerate(order):
                        if gk == g and name[0] == "L":
                            c, part = int(name[1]) // 2, int(name[1]) % 2
                            act.wait_ge(job_done, jobs_through(b, k))
                            w = (w_hi, w_lo)[part]
                            act.activation(w[:, bass.ds(b * WB + c * CH, CH)], ps_j[:, k % 2, 0:CH],
                                           ACT.Copy).then_inc(emptied["L"], 1)

            act.wait_ge(mem_rdy, 1)
            act.wait_ge(mrow_out, 2 * 16 * SLOTS)
            batches(act, body)
            take_out(4 * B - 1, 1, 2 * B - 1)

        @block.vector
        def _(dve):
            class Chain:
                base, per, b, k = 0, 0, 0, 0

            def link(ins):
                Chain.k += 1
                ins.then_inc(dv, 1)
                dve.wait_ge(dv, Chain.b * Chain.per + (Chain.base + Chain.k))

            dve.memset(mhalf[:], -0.5).then_inc(half_rdy, 1)

            def norm_stats(b):
                dve.wait_ge(inp, (b + 1) * 64)
                for t in range(2):
                    ins = dve.bn_stats(stats[:, t, :], x_in[:, t, :])
                link(ins)
                settle(dve, settled)
                for t in range(2):
                    ins = dve.bn_aggr(mv[:, t, :], stats[:, t, :])
                link(ins)
                dve.tensor_scalar(ve[:], mv[:, :, 1], EPS, None, ALU.add).then_inc(var_rdy, 1)

            def normalise(b, jobs):
                dve.wait_ge(rstd_rdy, b + 1)
                wait(dve, job_done, jobs)
                for t in range(2):
                    ins = dve.tensor_scalar(xn[:, t, :], x_in[:, t, :], mv[:, t, 0:1], rstd[:, t:t + 1],
                                            ALU.subtract, ALU.mult)
                ins.then_inc(xn_rdy, 1)

            def cut(parts, stage, cuts):
                if stage == 1:
                    dve.wait_ge(rounded, cuts * 2 + 1)
                    dve.tensor_tensor(rest[:], full[:], parts[:, 0, :], ALU.subtract).then_inc(rest_rdy, 1)
                if stage == 3:
                    dve.wait_ge(rounded, cuts * 2 + 2)
                    dve.tensor_tensor(parts[:, 2, :], rest[:], parts[:, 1, :], ALU.subtract
                                      ).then_inc(parts_rdy, 1)

            def take_q(b, par, half, job, slot):
                dve.wait_ge(job_done, job)
                dve.scalar_tensor_tensor(out=full[:], in0=ps_j[:, slot, :], scalar=b_sb[:, half:half + 1],
                                         in1=mb[:, par, :], op0=ALU.add, op1=ALU.mult).then_inc(emptied["q"], 1)

            def take_k(b, par, half, job, slot):
                dve.wait_ge(job_done, job)
                dve.scalar_tensor_tensor(out=full[:], in0=mb[:, par, :], scalar=b_sb[:, 2 + half:3 + half],
                                         in1=ps_j[:, slot, :], op0=ALU.mult, op1=ALU.add
                                         ).then_inc(emptied["k"], 1)

            def take_v(b, par, half, job, slot, j):
                if j == 0:
                    dve.wait_ge(job_done, job)
                    wait(dve, pv_done, (b - 1) * 16)
                ins = dve.scalar_tensor_tensor(
                    out=vt[:, par, half, j, :, 0:D],
                    in0=bv_b[:, half * P:(half + 1) * P].rearrange("p (h d) -> p h d", d=D),
                    scalar=mcol[:, par, j:j + 1],
                    in1=ps_j[:, slot, j * P:(j + 1) * P].rearrange("p (h d) -> p h d", d=D),
                    op0=ALU.mult, op1=ALU.add)
                if j == 3:
                    ins.then_inc(emptied["v"], 1)

            def take_max(n, g2, job, slot):
                dve.wait_ge(job_done, job)
                wait(dve, max_in, (n - 1) * 32)
                link(dve.tensor_scalar(mt[:, g2, 0, :], ps_j[0:16, slot, 0:P], -1.0, None, ALU.mult))
                dve.scalar_tensor_tensor(out=mt[:, g2, 1, :], in0=ps_j[0:16, slot, 0:P], scalar=-1.0,
                                         in1=mt[:, g2, 0, :], op0=ALU.mult, op1=ALU.subtract
                                         ).then_inc(emptied["T"], 1)

            def maxima(b, hb, i):
                m = 4 * hb + i
                dve.wait_ge(s_done, b * 64 + (m + 1))
                col = 4 * (hb % 4) + i
                dve.tensor_reduce(mx[:, (hb // 4) % 2, col:col + 1], ps_s[:, max_bank(m), :], X,
                                  ALU.max).then_inc(mx_done, 1)

            def hot(b, c, job, t):
                if t == 0:
                    dve.wait_ge(idxf_rdy, b * 4 + (c + 1))
                    wait(dve, job_done, job)
                ins = dve.tensor_scalar(onehot[:, c % 2, t, :, :], idxf[:, c % 2, :, :], entry[:, t:t + 1], None,
                                        ALU.is_equal)
                if t == LQ - 1:
                    ins.then_inc(hot_rdy, 1)

            def masked_inverse(b, par, half):
                u = b * 2 + half
                for p2 in range(2):
                    dve.wait_ge(gathered[p2], (u + 1) * GATHER)
                dve.wait_ge(tm_in, (b + 1) * 16)
                link(dve.reciprocal(rden[:, half, :], den[:, half, :]))
                wait(dve, bounce, (u - 1) * 16)
                dve.tensor_tensor(rden[:, half, :], rden[:, half, :], tm[:, par, :], ALU.mult
                                  ).then_inc(rden_rdy, 1)

            def prepare_table():
                dve.wait_ge(small_in, 16 * 5)
                link(dve.tensor_scalar(lut_b[:, 1, :], lut_b[:, 0, :], -1.0, None, ALU.mult))
                link(dve.tensor_tensor(lut_b[:, 2, :], lut_b[:, 0, :], lut_b[:, 1, :], ALU.max))
                link(dve.tensor_reduce(lt[:, 0:1], lut_b[:, 2, :], X, ALU.max))
                link(dve.tensor_scalar(lt[:, 1:2].bitcast(U32), lt[:, 0:1].bitcast(U32), 0x7F800000, None,
                                       ALU.bitwise_and))
                link(dve.tensor_scalar(lt[:, 2:3], lt[:, 1:2], 2.0 ** -100, None, ALU.max))
                link(dve.reciprocal(lt[:, 3:4], lt[:, 2:3]))
                link(dve.tensor_scalar(lt[:, 4:5], lt[:, 3:4], 2.0 ** 14, None, ALU.mult))
                link(dve.tensor_scalar(lut_q[:, 0, :], lut_q[:, 0, :], lt[:, 4:5], None, ALU.mult))
                link(dve.tensor_copy(lut16[:], lut_q[:, 0, :]))
                link(dve.tensor_copy(lut_q[:, 1, :], lut16[:]))
                link(dve.tensor_tensor(lut_q[:, 2, :], lut_q[:, 0, :], lut16[:], ALU.subtract))
                link(dve.tensor_scalar(scales[:, 0:1], lt[:, 2:3], 2.0 ** -25, None, ALU.mult))
                link(dve.tensor_scalar(scales[:, 1:2], lt[:, 3:4], 2.0 ** -30, None, ALU.mult))
                link(dve.tensor_scalar(lt[:, 5:6], lt[:, 2:3], lt[:, 2:3], None, ALU.mult))
                link(dve.tensor_scalar(lt[:, 6:7], lt[:, 5:6], lt[:, 2:3], None, ALU.mult))
                link(dve.tensor_scalar(scales[:, 2:3], lt[:, 6:7], 2.0 ** -9, None, ALU.mult))
                dve.wait_ge(ident_rdy, 2)
                link(dve.tensor_copy(ident16[:], ident[:]))
                for k in range(2):
                    link(dve.tensor_tensor(eye[:, k, :], ident[:, 2 * k * Q:(2 * k + 1) * Q],
                                           ident[:, (2 * k + 1) * Q:(2 * k + 2) * Q], ALU.add))
                link(dve.tensor_tensor(eye[:, 2, :], eye[:, 0, :], eye[:, 1, :], ALU.add))
                for a in range(4):
                    for t in range(LQ):
                        ins = dve.memset(entry[Q * a:Q * a + Q, t:t + 1], float(4 * t + a))
                link(ins)
                for part in range(2):
                    for t in range(LQ):
                        ins = dve.tensor_scalar(diag[:, part, t, :], eye[:, 2, :],
                                                lut_q[:, 1 + part, t:t + 1], None, ALU.mult)
                ins.then_inc(diag_rdy, 1)

            dve.memset(vt[:, :, :, :, :, D:DW], 1.0)
            dve.memset(ks[96:P, :, :, :].bitcast(U32), 0x3F803F80)
            dve.memset(ps_o[:], 0.0).then_inc(mem_rdy, 1)
            mrow, mres = num[0:B, 0, :], rb[0:B, :]
            dve.wait_ge(mask_in, 16)
            for side in range(2):
                if side == 1:
                    norm_stats(0)
                    normalise(0, 0)
                if side == 0:
                    link(dve.tensor_copy(mres, mrow))
                else:
                    link(dve.tensor_scalar(mres, mrow, -1.0, 4.0 * NEG, ALU.add, ALU.mult))
                mpart = o_sb[0:B, side, :].bitcast(BF16).rearrange("p (s t) -> p s t", t=T)
                for part in range(2):
                    link(dve.tensor_copy(mpart[:, part, :], mres))
                    link(dve.tensor_tensor(mres, mres, mpart[:, part, :], ALU.subtract))
                dve.tensor_copy(xr[0:B, :].bitcast(BF16)[:, side * T:(side + 1) * T], mres).then_inc(mparts_rdy, 1)
                dve.wait_ge(mparts_rdy, side + 1)
            dve.wait_ge(const_in, 16 * 6)
            for half in range(2):
                take_q(0, 0, half, 3 * half + 1, (3 * half + 1) % 2)
                for stage in range(4):
                    cut(qp, stage, 2 * half)
                take_k(0, 0, half, 3 * half + 2, (3 * half + 2) % 2)
                for stage in range(4):
                    cut(kp, stage, 2 * half + 1)
                for j in range(4):
                    take_v(0, 0, half, 3 * half + 3, (3 * half + 3) % 2, j)
                if half == 0:
                    prepare_table()
            for h in range(AHEAD):
                for i in range(4):
                    maxima(0, h, i)
                if h == 3:
                    take_max(0, 0, 7, 1)
            for c in range(2):
                for t in range(LQ):
                    hot(0, c, 0, t)
            Chain.base, Chain.per, Chain.k = Chain.k, LINKS, 0

            def body(b, par, load=True, last=False):
                order = jobs_of(last)
                Chain.b, Chain.k = b, 0
                last_of = {name: jobs_through(b, k) for k, (_, name) in enumerate(order)}
                for g in range(STEPS):
                    hb = g + AHEAD
                    for i in range(4):
                        if hb < H or not last:
                            maxima(b, hb, i)
                        for k, (gk, name) in enumerate(order):
                            if gk == g and name == "T" and i == 0:
                                take_max(b * 4 + (g // 4 + 1), (g // 4 + 1) % 2, jobs_through(b, k), k % 2)
                            if gk == g - 1 and name == "q":
                                cut(qp, i, b * 4 + (4 + 2 * (g // 8)))
                            if gk == g - 1 and name == "k":
                                cut(kp, i, b * 4 + (5 + 2 * (g // 8)))
                            if gk == g - 1 and name == "v" and i < 2:
                                for j in (2 * i, 2 * i + 1):
                                    take_v(b + 1, 1 - par, g // 8, jobs_through(b, k), k % 2, j)
                    for at, c, job in ((3, 2, "L1"), (7, 3, "L3"), (11, 0, "L5"), (15, 1, "L7")):
                        if g == at and (at < 8 or not last):
                            for t in range(LQ):
                                hot(b + at // 8, c, last_of[job], t)
                    for k, (gk, name) in enumerate(order):
                        if gk != g:
                            continue
                        job, half = jobs_through(b, k), g // 8
                        if name == "q":
                            take_q(b + 1, 1 - par, half, job, k % 2)
                        if name == "k":
                            take_k(b + 1, 1 - par, half, job, k % 2)
                    if g == 0 and not last:
                        norm_stats(b + 1)
                    if g == 2 and not last:
                        normalise(b + 1, jobs_through(b, -1))
                    if g == 4 and not (isinstance(b, int) and b == 0):
                        masked_inverse(b - 1, 1 - par, 1)
                    if g == 12:
                        masked_inverse(b, par, 0)
                if isinstance(b, int) and b == 0:
                    Chain.base -= LINKS - Chain.k

            batches(dve, body)
            Chain.base, Chain.b = Chain.base + LINKS * (B - 1) + Chain.k, 0
            Chain.k = 0
            masked_inverse(B - 1, 1, 1)

        @block.tensor
        def _(pe):
            def job_matmuls(b, name, g, slot):
                todo = []
                half = g // 8
                cols = slice(half * P, (half + 1) * P)
                if name in "qk":
                    w, src = (wq_sb, xn) if name == "q" else (wk_sb, cm)
                    for t in range(2):
                        todo.append((ps_j[:, slot, :], w[:, t, cols], src[:, t, :], t == 0, t == 1))
                if name == "v":
                    for j in range(4):
                        for t in range(2):
                            todo.append((ps_j[:, slot, j * P:(j + 1) * P], cm[:, t, j * P:(j + 1) * P],
                                         wv_sb[:, t, cols], t == 0, t == 1))
                if name[0] == "L":
                    c, part = int(name[1]) // 2, int(name[1]) % 2
                    for t in range(LQ):
                        for g in range(4):
                            todo.append((ps_j[Q * g:Q * g + Q, slot, 0:CH], diag[:, part, t, :],
                                         onehot[:, c % 2, t, g, :], t == 0, t == LQ - 1))
                return todo

            def run(todo, count):
                for _ in range(min(count, len(todo))):
                    dst, lhs, rhs, start, stop = todo.pop(0)
                    ins = pe.matmul(dst, lhs, rhs, start=start, stop=stop)
                    if not todo:
                        ins.then_inc(job_done, 1)

            def scores_for_max(b, hb, i):
                half, h = (hb // 8) % 2, hb % 8
                m = 4 * hb + i
                wait(pe, mx_done, b * 64 + (max_bank_before(m) + 1))
                pe.matmul(ps_s[:, max_bank(m), :], qs[0:XROW, half, h, i * P:(i + 1) * P],
                          ks[0:XROW, half, h, :], start=True, stop=True).then_inc(s_done, 1)

            def turn_max(n2, slot):
                pe.transpose(ps_j[0:16, slot, 0:P], mx[:, n2, :], ident[:]).then_inc(job_done, 1)

            def before_job(b, k, last, name):
                kind, through = ordinal(b, k - 2, last)
                pe.wait_ge(emptied[kind], through)
                if name == "q":
                    pe.wait_ge(xn_rdy, b + 2)
                if name in "kv":
                    pe.wait_ge(cm_rdy, b + 2)
                if name[0] == "L":
                    if isinstance(b, int) and b == 0:
                        pe.wait_ge(diag_rdy, 1)
                    pe.wait_ge(hot_rdy, b * 4 + (int(name[1]) // 2 + 1))

            def values(b, par, g):
                s, j = g // 4, g % 4
                half, h0 = s // 2, 4 * (s % 2)
                pe.wait_ge(exp_done, b * 64 + (4 * g + 4))
                if j == 0:
                    wait(pe, o_rdy, b * 4 + s)
                if g % 8 == 0:
                    pe.wait_ge(emptied["v"], b * 2 + (half + 1))
                for i in range(4):
                    ins = pe.matmul(ps_o[32 * i:32 * i + DW, :], vt[:, par, half, j, h0 + i, :],
                                    probs[:, g % 2, i, :], start=(j == 0), stop=(j == 3))
                ins.then_inc(pv_done, 1)

            pe.wait_ge(const_in, 16 * 6)
            pe.wait_ge(xn_rdy, 1)
            pe.wait_ge(cm_rdy, 1)
            for i, name in enumerate(FIRST[:6]):
                if i >= 2:
                    pe.wait_ge(emptied[FIRST[i - 2]], FIRST[:i - 1].count(FIRST[i - 2]))
                run(job_matmuls(0, name, 8 * (i // 3), (i + 1) % 2), 99)
            pe.wait_ge(mem_rdy, 1)
            pe.wait_ge(stack_in[0], NSTACK)
            pe.wait_ge(mask_set[0], 32)
            for h in range(AHEAD):
                for i in range(4):
                    scores_for_max(0, h, i)
                if h == 3:
                    pe.wait_ge(mx_done, 16)
                    pe.wait_ge(emptied["k"], 2)
                    turn_max(0, 1)

            def body(b, par, load=True, last=False):
                order = jobs_of(last)
                for g in range(STEPS):
                    s, j = g // 4, g % 4
                    half, h0 = s // 2, 4 * (s % 2)
                    hb = g + AHEAD
                    more = hb < H or not last
                    if hb == 8:
                        pe.wait_ge(stack_in[1], (b + 1) * NSTACK)
                        pe.wait_ge(mask_set[1], (b + 1) * 32)
                    if hb == 16 and more:
                        pe.wait_ge(stack_in[0], (b + 2) * NSTACK)
                        pe.wait_ge(mask_set[0], (b + 2) * 32)
                    todo, mine = [], [(k, name) for k, (gk, name) in enumerate(order) if gk == g]
                    first = 2 if len(mine) > 1 else 0
                    for i in range(4):
                        m = 4 * g + i
                        if more and j == 0:
                            for ahead in ((0, 1, 2), (3,), (), ())[i]:
                                scores_for_max(b, hb, ahead)
                        if j == 0 and i == 0:
                            if g > 0:
                                values(b, par, g - 1)
                            elif not (isinstance(b, int) and b == 0):
                                values(b - 1, 1 - par, STEPS - 1)
                            pe.wait_ge(max_in, (b * 4 + (s + 1)) * 32)
                        wait(pe, exp_done, b * 64 + (m - 1))
                        pe.matmul(ps_t[:, m % 2, :], ks[0:SROWS, half, h0 + i, j * P:(j + 1) * P],
                                  qs[0:SROWS, half, h0 + i, :], start=True, stop=True).then_inc(t_done, 1)
                        if more and j > 0:
                            scores_for_max(b, hb, i)
                        for k, name in mine:
                            if name == "T":
                                if i == 1:
                                    before_job(b, k, last, name)
                                    pe.wait_ge(mx_done, (b * 4 + (s + 2)) * 16)
                                    turn_max((s + 1) % 2, k % 2)
                            elif i >= first:
                                if i == first:
                                    before_job(b, k, last, name)
                                    todo = job_matmuls(b, name, g, k % 2)
                                    total = len(todo)
                                unit = 4 if name[0] == "L" else 1
                                share = lambda q: q * total // (4 - first) // unit * unit
                                run(todo, share(i + 1 - first) - share(i - first))
                        if i == 0 and j > 0:
                            values(b, par, g - 1)

            batches(pe, body)
            values(B - 1, 1, STEPS - 1)


GATHER = 16 * 5
LINKS = 2 + 4 + 2


def ffn(nc, st, xmid, out, w_hi, w_lo, scales, ident16):
    def sb(name, shape, dt=F32):
        return st.enter_context(nc.sbuf_tensor(name, shape, dt))

    def sem(name):
        return st.enter_context(nc.semaphore(name))

    NG = B * C // GT
    xg = sb("xg", [P, 2, GTT, T])
    xs = sb("xs", [P, 2, T])
    xh = sb("xh", [P, GTT, 2, T], F16)
    xt = sb("xt", [P, 2, 2, KT, GT], F16)
    sil = sb("sil", [P, 2, GT])
    hf = sb("hf", [P, 2, GT])
    ht = sb("ht", [P, IT, 2, GT], F16)
    res = sb("res", [P, 2, T])
    stats = sb("f_stats", [P, GTT, 6])
    mv = sb("f_mv", [P, GTT, 2])
    ve = sb("f_ve", [P, GTT])
    mhalf = sb("f_mhalf", [P, GTT])
    rstd = sb("f_rstd", [P, GTT])
    ps_g = st.enter_context(nc.psum_tensor("ps_g", [P, 2, 512], F32))
    ps_u = st.enter_context(nc.psum_tensor("ps_u", [P, 2, 512], F32))
    ps_d = st.enter_context(nc.psum_tensor("ps_d", [P, 2, 512], F32))
    ps_x = st.enter_context(nc.psum_tensor("ps_x", [P, 2, 1024], F16))

    settled = sem("f_settled")
    x_sem = sem("f_x_in")
    half_rdy = sem("f_half_rdy")
    var_rdy = sem("f_var_rdy")
    rstd_rdy = sem("f_rstd_rdy")
    xs_rdy = sem("f_xs_rdy")
    fdv = sem("f_dv")
    xh_rdy = sem("f_xh_rdy")
    turned = sem("f_turned")
    xt_rdy = sem("f_xt_rdy")
    gate_done = sem("f_gate_done")
    up_done = sem("f_up_done")
    sil_rdy = sem("f_sil_rdy")
    h_rdy = sem("f_h_rdy")
    ht_rdy = sem("f_ht_rdy")
    down_done = sem("f_down_done")
    res_rdy = sem("f_res_rdy")
    stored = [sem("f_stored0"), sem("f_stored1")]

    def width(i):
        return P if i < IT - 1 else ILAST

    def groups(eng, body):
        body(0, 0)
        body(1, 1)
        with eng.Fori(1, NG // 2 - 1) as pair:
            body(pair * 2, 0)
            body(pair * 2 + 1, 1)
        body(NG - 2, 0)
        body(NG - 1, 1, last=True)

    per_group = GT // C
    rows = lambda a, n: a[bass.ds(n * per_group, per_group), :, :].rearrange("b (t p) f -> p (b t) f", p=P)

    with nc.Block() as block:

        @block.sync
        def _(sp):
            sp.dma_start(xg[:, 0, :, :], rows(xmid, 0)).then_inc(x_sem, 16)

            def body(n, par, last=False):
                if not last:
                    wait(sp, res_rdy, n * GTT)
                    settle(sp, settled)
                    sp.wait_ge(xs_rdy, (n + 1) * GTT)
                    settle(sp, settled)
                    sp.dma_start(xg[:, 1 - par, :, :], rows(xmid, n + 1)).then_inc(x_sem, 16)
                for t in range(GTT):
                    sp.wait_ge(res_rdy, n * GTT + (t + 1))
                    settle(sp, settled)
                    b, r = n * per_group + t // 2, (t % 2) * P
                    sp.dma_start(out[bass.ds(b, 1), r:r + P, :].rearrange("o p f -> (o p) f"),
                                 res[:, t % 2, :]).then_inc(stored[t % 2], 16)

            groups(sp, body)
            for q in stored:
                sp.wait_ge(q, 16 * NG * GTT // 2)

        @block.gpsimd
        def _(pool):
            pool.memset(mhalf[:], -0.5).then_inc(half_rdy, 1)
            pool.wait_ge(half_rdy, 1)

            def inv_std(n):
                pool.wait_ge(var_rdy, n + 1)
                pool.tensor_tensor(rstd[:], ve[:], mhalf[:], ALU.pow).then_inc(rstd_rdy, 1)

            inv_std(0)

            def body(n, par, last=False):
                if not last:
                    inv_std(n + 1)

            groups(pool, body)

        @block.scalar
        def _(act):
            def take_turned(n, par):
                for t in range(GTT):
                    act.wait_ge(turned, n * GTT + (t + 1))
                    act.activation(xt[:, par, :, :, t * P:(t + 1) * P],
                                   ps_x[:, t % 2, :].rearrange("p (a k t) -> p a k t", a=2, k=KT),
                                   ACT.Copy).then_inc(xt_rdy, 1)

            take_turned(0, 0)

            def body(n, par, last=False):
                for i in range(IT):
                    w = width(i)
                    act.wait_ge(gate_done, n * IT + (i + 1))
                    wait(act, h_rdy, n * IT + (i - 1))
                    act.activation(sil[0:w, i % 2, :], ps_g[0:w, i % 2, :], ACT.Silu,
                                   scale=scales[0:w, 0:1]).then_inc(sil_rdy, 1)
                if not last:
                    take_turned(n + 1, 1 - par)

            groups(act, body)

        @block.vector
        def _(dve):
            def norm(n, par):
                dve.wait_ge(x_sem, (n + 1) * 16)
                for t in range(GTT):
                    ins = dve.bn_stats(stats[:, t, :], xg[:, par, t, :])
                ins.then_inc(fdv, 1)
                dve.wait_ge(fdv, n * 2 + 1)
                settle(dve, settled)
                for t in range(GTT):
                    ins = dve.bn_aggr(mv[:, t, :], stats[:, t, :])
                ins.then_inc(fdv, 1)
                dve.wait_ge(fdv, n * 2 + 2)
                dve.tensor_scalar(ve[:], mv[:, :, 1], EPS, 2.0 ** -22, ALU.add, ALU.mult).then_inc(var_rdy, 1)

            def parts(n, par):
                dve.wait_ge(rstd_rdy, n + 1)
                wait(dve, turned, n * GTT)
                for t in range(GTT):
                    dve.tensor_scalar(xs[:, t % 2, :], xg[:, par, t, :], mv[:, t, 0:1], rstd[:, t:t + 1],
                                      ALU.subtract, ALU.mult).then_inc(xs_rdy, 1)
                    dve.wait_ge(xs_rdy, n * GTT + (t + 1))
                    dve.tensor_copy(xh[:, t, 0, :], xs[:, t % 2, :]).then_inc(xh_rdy, 1)
                    dve.wait_ge(xh_rdy, (n * GTT + t) * 2 + 1)
                    dve.tensor_tensor(xh[:, t, 1, :], xs[:, t % 2, :], xh[:, t, 0, :], ALU.subtract
                                      ).then_inc(xh_rdy, 1)

            norm(0, 0)
            parts(0, 0)

            def body(n, par, last=False):
                for i in range(IT):
                    w = width(i)
                    dve.wait_ge(sil_rdy, n * IT + (i + 1))
                    dve.wait_ge(up_done, n * IT + (i + 1))
                    if i == 0:
                        wait(dve, down_done, n * GTT)
                    dve.scalar_tensor_tensor(out=hf[0:w, i % 2, :], in0=sil[0:w, i % 2, :],
                                             scalar=scales[0:w, 1:2], in1=ps_u[0:w, i % 2, :],
                                             op0=ALU.mult, op1=ALU.mult).then_inc(h_rdy, 1)
                    dve.wait_ge(h_rdy, n * IT + (i + 1))
                    dve.tensor_copy(ht[0:w, i, 0, :], hf[0:w, i % 2, :]).then_inc(ht_rdy, 1)
                    dve.wait_ge(ht_rdy, (n * IT + i) * 2 + 1)
                    dve.tensor_tensor(ht[0:w, i, 1, :], hf[0:w, i % 2, :], ht[0:w, i, 0, :], ALU.subtract
                                      ).then_inc(ht_rdy, 1)
                    if i == 6 and not last:
                        norm(n + 1, 1 - par)
                    if i == 7 and not last:
                        parts(n + 1, 1 - par)
                for t in range(GTT):
                    dve.wait_ge(down_done, n * GTT + (t + 1))
                    wait(dve, stored[t % 2], (n * 2 + t // 2) * 16)
                    dve.scalar_tensor_tensor(out=res[:, t % 2, :], in0=ps_d[:, t % 2, :],
                                             scalar=scales[:, 2:3], in1=xg[:, par, t, :],
                                             op0=ALU.mult, op1=ALU.add).then_inc(res_rdy, 1)

            groups(dve, body)

        @block.tensor
        def _(pe):
            def turn(n, par):
                for t in range(GTT):
                    pe.wait_ge(xh_rdy, (n * GTT + (t + 1)) * 2)
                    wait(pe, xt_rdy, n * GTT + (t - 1))
                    for part in range(2):
                        for k in range(KT):
                            c = (part * KT + k) * P
                            ins = pe.transpose(ps_x[:, t % 2, c:c + P], xh[:, t, part, k * P:(k + 1) * P],
                                               ident16[:])
                    ins.then_inc(turned, 1)

            turn(0, 0)

            def body(n, par, last=False):
                pe.wait_ge(xt_rdy, (n + 1) * GTT)
                for i in range(IT):
                    w = width(i)
                    for base, ps, done, free in ((GATE0, ps_g, gate_done, sil_rdy), (UP0, ps_u, up_done, h_rdy)):
                        wait(pe, free, n * IT + (i - 1))
                        for k in range(KT):
                            c = base + k * INTER + i * P
                            for wp, part in ((w_hi, 0), (w_hi, 1), (w_lo, 0)):
                                first, end = k == 0 and wp is w_hi and part == 0, k == KT - 1 and wp is w_lo
                                ins = pe.matmul(ps[0:w, i % 2, :], wp[:, c:c + w], xt[:, par, part, k, :],
                                                start=first, stop=end)
                        ins.then_inc(done, 1)
                if not last:
                    turn(n + 1, 1 - par)
                pe.wait_ge(ht_rdy, (n + 1) * (2 * IT))
                for t in range(GTT):
                    wait(pe, res_rdy, n * GTT + (t - 1))
                    for i in range(IT):
                        w = width(i)
                        c = DOWN0 + i * T
                        for wp, part in ((w_hi, 0), (w_lo, 0), (w_hi, 1)):
                            ins = pe.matmul(ps_d[:, t % 2, :], ht[0:w, i, part, t * P:(t + 1) * P],
                                            wp[0:w, c:c + T], start=(i == 0 and wp is w_hi and part == 0),
                                            stop=(i == IT - 1 and part == 1))
                    ins.then_inc(down_done, 1)

            groups(pe, body)


def kernel(x, ctx_2048, mask_Bx1x2048_fk1, L0_xattn_Wq, L0_xattn_bq, L0_xattn_Wk, L0_xattn_bk, L0_xattn_Wv,
           L0_xattn_bv, L0_ffn_lut, L0_ffn_gate_idx, L0_ffn_up_idx, L0_ffn_down_idx):
    import numpy as np
    import concourse.bacc as bacc
    from concourse.bass_utils import run_bass_kernel_spmd

    c = np.ascontiguousarray
    a = lambda v: np.asarray(v)

    def tiles(i):
        t = a(i).T
        pad = -t.shape[0] % P
        t = np.pad(t, ((0, pad), (0, 0)))
        return t.reshape(-1, P, t.shape[1]).transpose(1, 0, 2).reshape(P, -1)

    def by_row(v):
        v = a(v)
        return v.reshape(2, H // 2, D, -1).transpose(0, 2, 1, 3).reshape(v.shape)

    def spread(i):
        i = i.reshape(4, Q, B, 4, CH).transpose(2, 3, 1, 0, 4)
        return c(np.broadcast_to(i[:, :, None], (B, 4, 4, Q, 4, CH)).reshape(B, 4, P, 4, CH))

    idx = np.concatenate([tiles(L0_ffn_gate_idx), tiles(L0_ffn_up_idx), tiles(L0_ffn_down_idx)], axis=1)
    arrays = {
        "x": a(x), "ctx": a(ctx_2048), "mask": a(mask_Bx1x2048_fk1),
        "wq": c(by_row(L0_xattn_Wq).T), "bq": c(by_row(L0_xattn_bq).reshape(2, P).T),
        "wk": c(by_row(L0_xattn_Wk).T), "bk": c(by_row(L0_xattn_bk).reshape(2, P).T),
        "wv": c(a(L0_xattn_Wv).T), "bv": c(a(L0_xattn_bv).reshape(1, C)),
        "lut": c(a(L0_ffn_lut).reshape(1, LUT)), "idx": spread(idx),
    }
    nc = bacc.Bacc("TRN2", target_bir_lowering=False, num_devices=1)
    args = [nc.dram_tensor(n, v.shape, mybir.dt.from_np(v.dtype), kind="ExternalInput").ap()
            for n, v in arrays.items()]
    out = nc.dram_tensor("out", [B, C, T], F32, kind="ExternalOutput").ap()
    build(nc, *args, out)
    r = run_bass_kernel_spmd(nc, [arrays], core_ids=[0])
    return r.results[0]["out"]
```
